# Optimizing a Trainium2 kernel written in Bass

```python
import numpy as np
import jax
import jax.numpy as jnp

def _softmax(x, axis=-1):
    return jax.nn.softmax(x, axis=axis)
def _gelu(x):
    return jax.nn.gelu(x, approximate=True)
def _silu(x):
    return jax.nn.silu(x)
def _sigmoid(x):
    return jax.nn.sigmoid(x)
def _layernorm(x, axis=-1, eps=1e-5):
    m = jnp.mean(x, axis=axis, keepdims=True)
    v = jnp.var(x, axis=axis, keepdims=True)
    return (x - m) / jnp.sqrt(v + eps)
def _scatter_add(tgt, idx, src, axis=0):
    return tgt.at[idx].add(src)
def _segment_sum(src, seg, n):
    return jax.ops.segment_sum(src, seg, n)

kernel_name = 'mk_conv_preact_d2_conv_nchw192_e01f03'

def setup_inputs(seed: int = 0):
    np.random.seed(seed)
    _w = jnp.asarray
    def _rec_inputs():
        import jax
        import jax.numpy as jnp
        _gk = jax.random.key(seed)
        x = -0.0002221 + 1 * jax.random.normal(jax.random.fold_in(_gk, 1), (8, 192, 128, 128), jnp.float32)
        return x
    x = _rec_inputs()
    def _L0_conv_setup():
        import jax, jax.numpy as jnp
        import numpy as np
        DIM = 192
        HEADS = 4
        EPS = 1e-12

        def _custom_normalize(t):
            norm = jnp.sqrt(jnp.sum(t * t, axis=-1, keepdims=True)) + EPS
            return t / norm

        def _f_normalize(t):
            norm = jnp.sqrt(jnp.sum(t * t, axis=-1, keepdims=True))
            return t / jnp.maximum(norm, EPS)
        key = jax.random.key(seed)
        ks = jax.random.split(key, 5)
        b, c, h, w = (8, DIM, 128, 128)
        x = jax.random.normal(ks[0], (b, c, h, w), dtype=jnp.float32)
        w_qkv = jax.random.normal(ks[1], (3 * c, c), dtype=jnp.float32) * (1.0 / np.sqrt(c))
        w_dw = jax.random.normal(ks[2], (3 * c, 1, 3, 3), dtype=jnp.float32) * (1.0 / 3.0)
        w_proj = jax.random.normal(ks[3], (c, c), dtype=jnp.float32) * (1.0 / np.sqrt(c))
        temperature = jnp.ones((HEADS, 1, 1), dtype=jnp.float32)
        return {'x': x, 'w_qkv': w_qkv, 'w_dw': w_dw, 'w_proj': w_proj, 'temperature': temperature}
    _L0_conv_all = _L0_conv_setup()
    _L0_conv_in = {k: v for k, v in _L0_conv_all.items() if k in ('w_qkv', 'w_dw', 'w_proj', 'temperature', )}
    del _L0_conv_all

    def _L1_conv_setup():
        import jax, jax.numpy as jnp
        import numpy as np
        FILTERS = (1, 3, 3, 3, 1)
        INIT_SCALE = 10.0
        BOUND = 1e-06

        @jax.custom_vjp
        def low_bound(x):
            return jnp.maximum(x, BOUND)

        def _lb_fwd(x):
            return (jnp.maximum(x, BOUND), x)

        def _lb_bwd(x, g):
            keep = jnp.logical_or(x >= BOUND, g < 0.0)
            return (g * keep.astype(g.dtype),)
        low_bound.defvjp(_lb_fwd, _lb_bwd)

        def _logits_cumulative(logits, ms, bs, fs):
            for i in range(4):
                logits = jnp.einsum('cof,cfn->con', jax.nn.softplus(ms[i]), logits) + bs[i]
                if i < 3:
                    logits = logits + jnp.tanh(fs[i]) * jnp.tanh(logits)
            return logits
        key = jax.random.key(seed)
        ks = jax.random.split(key, 16)
        B, C, H, W = (16, 192, 64, 64)
        scale = INIT_SCALE ** (1.0 / (len(FILTERS) - 1))
        inp = {'x_quant': jax.random.normal(ks[0], (B, C, H, W), jnp.float32) * 3.0}
        for i in range(4):
            fo, fi = (FILTERS[i + 1], FILTERS[i])
            init = float(np.log(np.expm1(1.0 / scale / fo)))
            inp[f'm{i}'] = init + 0.01 * jax.random.normal(ks[1 + i], (C, fo, fi), jnp.float32)
            inp[f'b{i}'] = jax.random.uniform(ks[5 + i], (C, fo, 1), jnp.float32, -0.5, 0.5)
            if i < 3:
                inp[f'f{i}'] = 0.1 * jax.random.normal(ks[9 + i], (C, fo, 1), jnp.float32)
        return inp
    _L1_conv_all = _L1_conv_setup()
    _L1_conv_in = {k: v for k, v in _L1_conv_all.items() if k in ('m0', 'm1', 'm2', 'm3', 'b0', 'b1', 'b2', 'b3', 'f0', 'f1', 'f2', )}
    del _L1_conv_all

    return {
        "x": x,
        "L0_conv_w_qkv": _L0_conv_in["w_qkv"],
        "L0_conv_w_dw": _L0_conv_in["w_dw"],
        "L0_conv_w_proj": _L0_conv_in["w_proj"],
        "L0_conv_temperature": _L0_conv_in["temperature"],
        "L1_conv_m0": _L1_conv_in["m0"],
        "L1_conv_m1": _L1_conv_in["m1"],
        "L1_conv_m2": _L1_conv_in["m2"],
        "L1_conv_m3": _L1_conv_in["m3"],
        "L1_conv_b0": _L1_conv_in["b0"],
        "L1_conv_b1": _L1_conv_in["b1"],
        "L1_conv_b2": _L1_conv_in["b2"],
        "L1_conv_b3": _L1_conv_in["b3"],
        "L1_conv_f0": _L1_conv_in["f0"],
        "L1_conv_f1": _L1_conv_in["f1"],
        "L1_conv_f2": _L1_conv_in["f2"],
    }

def reference(x, L0_conv_w_qkv, L0_conv_w_dw, L0_conv_w_proj, L0_conv_temperature, L1_conv_m0, L1_conv_m1, L1_conv_m2, L1_conv_m3, L1_conv_b0, L1_conv_b1, L1_conv_b2, L1_conv_b3, L1_conv_f0, L1_conv_f1, L1_conv_f2):
    import jax
    import jax.numpy as jnp
    def _L0_conv_ref(x, w_qkv, w_dw, w_proj, temperature):
        import jax, jax.numpy as jnp
        import numpy as np
        DIM = 192
        HEADS = 4
        EPS = 1e-12

        def _custom_normalize(t):
            norm = jnp.sqrt(jnp.sum(t * t, axis=-1, keepdims=True)) + EPS
            return t / norm

        def _f_normalize(t):
            norm = jnp.sqrt(jnp.sum(t * t, axis=-1, keepdims=True))
            return t / jnp.maximum(norm, EPS)
        b, c, h, w = x.shape
        c_fix = c // HEADS
        qkv = jnp.einsum('oc,bchw->bohw', w_qkv, x)
        qkv = jax.lax.conv_general_dilated(qkv, w_dw, window_strides=(1, 1), padding=((1, 1), (1, 1)), dimension_numbers=('NCHW', 'OIHW', 'NCHW'), feature_group_count=3 * c)
        q, k, v = jnp.split(qkv, 3, axis=1)
        q = q.reshape(b, HEADS, c_fix, h * w)
        k = k.reshape(b, HEADS, c_fix, h * w)
        v = v.reshape(b, HEADS, c_fix, h * w)
        q = _f_normalize(_custom_normalize(q))
        k = _f_normalize(_custom_normalize(k))
        attn = jnp.einsum('bhcn,bhdn->bhcd', q, k) * temperature
        attn = jax.nn.softmax(attn, axis=-1)
        out = jnp.einsum('bhcd,bhdn->bhcn', attn, v)
        out = out.reshape(b, c, h, w)
        out = jnp.einsum('oc,bchw->bohw', w_proj, out)
        return out

    def _L1_conv_ref(x_quant, m0, m1, m2, m3, b0, b1, b2, b3, f0, f1, f2):
        import jax, jax.numpy as jnp
        import numpy as np
        FILTERS = (1, 3, 3, 3, 1)
        INIT_SCALE = 10.0
        BOUND = 1e-06

        @jax.custom_vjp
        def low_bound(x):
            return jnp.maximum(x, BOUND)

        def _lb_fwd(x):
            return (jnp.maximum(x, BOUND), x)

        def _lb_bwd(x, g):
            keep = jnp.logical_or(x >= BOUND, g < 0.0)
            return (g * keep.astype(g.dtype),)
        low_bound.defvjp(_lb_fwd, _lb_bwd)

        def _logits_cumulative(logits, ms, bs, fs):
            for i in range(4):
                logits = jnp.einsum('cof,cfn->con', jax.nn.softplus(ms[i]), logits) + bs[i]
                if i < 3:
                    logits = logits + jnp.tanh(fs[i]) * jnp.tanh(logits)
            return logits
        B, C, H, W = x_quant.shape
        ms, bs, fs = ((m0, m1, m2, m3), (b0, b1, b2, b3), (f0, f1, f2))
        xq = jnp.transpose(x_quant, (1, 0, 2, 3)).reshape(C, 1, -1)
        lower = _logits_cumulative(xq - 0.5, ms, bs, fs)
        upper = _logits_cumulative(xq + 0.5, ms, bs, fs)
        sign = jax.lax.stop_gradient(-jnp.sign(lower + upper))
        likelihood = jnp.abs(jax.nn.sigmoid(sign * upper) - jax.nn.sigmoid(sign * lower))
        likelihood = low_bound(likelihood)
        return jnp.transpose(likelihood.reshape(C, B, H, W), (1, 0, 2, 3))

    def _gn(v, G=32, eps=1e-5):
        B_, C_, H_, W_ = v.shape
        g = v.reshape(B_, G, C_ // G, H_, W_)
        m = jnp.mean(g, axis=(2, 3, 4), keepdims=True)
        s = jnp.var(g, axis=(2, 3, 4), keepdims=True)
        return ((g - m) / jnp.sqrt(s + eps)).reshape(v.shape)

    def _ln_c(v, eps=1e-6):
        m = jnp.mean(v, axis=1, keepdims=True)
        s = jnp.var(v, axis=1, keepdims=True)
        return (v - m) / jnp.sqrt(s + eps)

    def _ln_t(v, eps=1e-5):
        m = jnp.mean(v, axis=-1, keepdims=True)
        s = jnp.var(v, axis=-1, keepdims=True)
        return (v - m) / jnp.sqrt(s + eps)

    def _to_tokens(v):
        B_, C_, H_, W_ = v.shape
        return v.reshape(B_, C_, H_ * W_).transpose(0, 2, 1)
    def _from_tokens(t, like):
        B_, C_, H_, W_ = like.shape
        return t.transpose(0, 2, 1).reshape(B_, C_, H_, W_)

    x = x + _L0_conv_ref(_gn(x), L0_conv_w_qkv, L0_conv_w_dw, L0_conv_w_proj, L0_conv_temperature)
    x = x + _L1_conv_ref(_gn(x), L1_conv_m0, L1_conv_m1, L1_conv_m2, L1_conv_m3, L1_conv_b0, L1_conv_b1, L1_conv_b2, L1_conv_b3, L1_conv_f0, L1_conv_f1, L1_conv_f2)
    return x


_drawn_inputs = setup_inputs


def setup_inputs(seed=0):
    import zlib

    import numpy as np

    out = dict(_drawn_inputs(seed))
    spreads = {'L0_conv_temperature': (1.0, 0.6)}
    factors = {'L1_conv_m0': 8.0,
     'L1_conv_m1': 8.0,
     'L1_conv_m2': 8.0,
     'L1_conv_m3': 8.0,
     'L1_conv_b0': 8.0,
     'L1_conv_b1': 8.0,
     'L1_conv_b2': 8.0,
     'L1_conv_b3': 8.0,
     'L1_conv_f0': 8.0,
     'L1_conv_f1': 8.0,
     'L1_conv_f2': 8.0}
    for name, (base, spread) in spreads.items():
        noise = np.random.default_rng([zlib.crc32(name.encode()), seed]).standard_normal(out[name].shape)
        drawn = base * np.exp(spread * noise) if base else spread * noise
        out[name] = jnp.asarray(drawn.astype(out[name].dtype))
    for name, factor in factors.items():
        out[name] = (out[name] * factor).astype(out[name].dtype)
    return out
```

```python
import concourse.bass as bass
from concourse import mybir
from contextlib import ExitStack

F32 = mybir.dt.float32
ACT = mybir.ActivationFunctionType
ALU = mybir.AluOpType
AX = mybir.AxisListType

NB, C, H, W = 8, 192, 128, 128
NPX = H * W
CA, CB = 128, C - 128
HEADS = 4
CH = C // HEADS
RB = 8
BLK = RB * W
NBLK = H // RB
PW = W + 2
NT = 4
TAPS = [0, 1, 2, 3, 5, 6, 7, 8]
HALF = 512
GN_EPS = 1e-5
EPS = 1e-12

G = 42
GP = 3 * G
ROWS = NB * C
NG = -(-ROWS // G)
GLAST = ROWS - (NG - 1) * G
TW = 3 * HALF
NIT = -(-NPX // TW)
LASTC = (NPX - (NIT - 1) * TW) // HALF
NU = 2 * NIT
NPAR = 15
BOUND = 1e-6


def build(nc, x, wqkv, wdw, wproj, temp, grp, ident_in, diag_in, par, out):
    v_dram = nc.dram_tensor("v_scratch", (NB, C, NPX), F32, kind="Internal").ap()
    x1_dram = nc.dram_tensor("x1_scratch", (ROWS, NPX), F32, kind="Internal").ap()
    st_dram = nc.dram_tensor("stats_scratch", (NG * G, 2), F32, kind="Internal").ap()

    ctx = ExitStack()
    with ctx:
        def sem(name):
            return ctx.enter_context(nc.semaphore(name))

        ps = ctx.enter_context(nc.psum_tensor("ps", [128, 8, HALF], F32))
        zt = ctx.enter_context(nc.sbuf_tensor("zt", [128, 4 * PW], F32))
        ident = ctx.enter_context(nc.sbuf_tensor("ident", [128, 128], F32))
        diag = ctx.enter_context(nc.sbuf_tensor("diag", [GP, G], F32))

        l0 = ExitStack()

        def sb0(name, shape):
            return l0.enter_context(nc.sbuf_tensor(name, shape, F32))

        wq_a, wq_b = sb0("wq_a", [CA, 640]), sb0("wq_b", [CB, 640])
        ws_a, ws_b = sb0("ws_a", [CA, 640]), sb0("ws_b", [CB, 640])
        dwc = sb0("dwc", [128, 5, 9])
        band = sb0("band", [128, 6, 128])
        grp_a, grp_b = sb0("grp_a", [CA, 256]), sb0("grp_b", [CB, 256])
        wp = sb0("wp", [CH, HEADS, C])
        tmp_bc = sb0("temp_bc", [CH, HEADS])
        xa, xb = sb0("xa", [CA, 2, BLK]), sb0("xb", [CB, 2, BLK])
        xra, xrb = sb0("xra", [CA, W]), sb0("xrb", [CB, W])
        pbuf = sb0("pbuf", [128, 2, NT, RB + 2, PW])
        p4 = sb0("p4", [128, 2, RB // 2 + 1, PW])
        acc = sb0("acc", [128, 2, NT, BLK])
        acc4 = sb0("acc4", [128, 2, BLK // 2])
        qkt = sb0("qkt", [128, 2, 384])
        va, vb = sb0("va", [CA, 2, BLK]), sb0("vb", [CB, 2, BLK])
        oa, ob = sb0("oa", [CA, 2, BLK]), sb0("ob", [CB, 2, BLK])
        bs_a, bs_b = sb0("bs_a", [CA, 2 * NBLK, 6]), sb0("bs_b", [CB, 2 * NBLK, 6])
        mv = sb0("mv", [128, 2, 2])
        gs = sb0("gs", [128, 8, 2])
        bias = sb0("bias", [128, 5])
        gram = sb0("gram", [96, HEADS, 96])
        gtmp = sb0("gtmp", [96, HEADS, 96])
        nrm = sb0("nrm", [96, 8, HEADS])
        at = sb0("at", [CH, 3, HEADS, CH])
        apad = sb0("apad", [CH, HEADS, C])
        pt_a, pt_b = sb0("pt_a", [CA, C]), sb0("pt_b", [CB, C])
        l0.close()

        def sb1(name, shape):
            return ctx.enter_context(nc.sbuf_tensor(name, shape, F32))

        tab = sb1("tab", [GP, NG, NPAR])
        sta = sb1("sta", [GP, NG, 2])
        lin = sb1("lin", [GP, NG, 3])
        w1t = sb1("w1t", [GP, NG, 3])
        wrk = sb1("wrk", [GP, NG, 2])
        sp_e, sp_u, sp_l, sp_m = (sb1(n, [GP, NG, 8]) for n in ("sp_e", "sp_u", "sp_l", "sp_m"))
        cur = sb1("cur", [GP, 3 + 3 + NPAR])
        cst = sb1("cst", [GP, 8])
        bd1 = sb1("bd1", [GP, GP])
        w1 = sb1("w1", [GP, GP])
        w2 = sb1("w2", [GP, GP])
        w3 = sb1("w3", [GP, 4, GP])
        xr = sb1("xr", [GP, 2, TW])
        xd = sb1("xd", [GP, 2, HALF])
        t0b = sb1("t0b", [GP, 2, TW])
        t12 = sb1("t12", [GP, 2, TW])
        zb = sb1("zb", [GP, 2, TW])
        hb = sb1("hb", [GP, 2, TW])
        lo_c, up_c = sb1("lo_c", [GP, HALF]), sb1("up_c", [GP, HALF])
        ssum, sgn = sb1("ssum", [GP, HALF]), sb1("sgn", [GP, HALF])
        sul = sb1("sul", [GP, 2, HALF])
        sig = sb1("sig", [GP, 2, HALF])
        dif = sb1("dif", [GP, HALF])
        lik = sb1("lik", [GP, HALF])
        res = sb1("res", [GP, 2, HALF])

        def c1set(s):
            return ps[:, 2 * s:2 * s + 2, :]
        T4O, TR, GR = 4, 5, 7
        PA, PB, PC = 0, 3, 6

        w_loaded = sem("w_loaded")
        zeroed = sem("zeroed")
        band_ready = sem("band_ready")
        x_loaded = [sem("x_loaded0"), sem("x_loaded1")]
        v_loaded = [sem("v_loaded0"), sem("v_loaded1")]
        row_loaded = sem("row_loaded")
        st_done = [sem("st_done0"), sem("st_done1")]
        c1_ready, evac_done = sem("c1_ready"), sem("evac_done")
        halo_done, tap_done = sem("halo_done"), sem("tap_done")
        dw_chain = sem("dw_chain")
        t4_done = [sem("t4_done0"), sem("t4_done1")]
        t4_evac = [sem("t4_evac0"), sem("t4_evac1")]
        tr_done = [sem("tr_done0"), sem("tr_done1")]
        tr_evac, gr_done = sem("tr_evac"), sem("gr_done")
        v_stored = [sem("v_stored0"), sem("v_stored1")]
        v4_stored = [sem("v4_stored0"), sem("v4_stored1")]
        ya_ready, yb_ready = sem("ya_ready"), sem("yb_ready")
        ya_done, yb_done = sem("ya_done"), sem("yb_done")
        y_stats = sem("y_stats")
        x1_stored = [sem("x1_stored0"), sem("x1_stored1")]
        gsteps = ["mv_marked", "mv_ready", "mg_ready", "dev_ready", "dsq_ready", "q_ready", "vg_ready", "ve_ready",
                  "sd_ready", "rstd_ready"]
        gx = {k: sem("gx_" + k) for k in gsteps}
        gy = {k: sem("gy_" + k) for k in gsteps}
        ws_ready, bias_ps, bias_ready = sem("ws_ready"), sem("bias_ps"), sem("bias_ready")
        stat_stored = sem("stat_stored")
        A = {k: sem("at_" + k) for k in [
            "gram", "diag", "n2", "n", "ne", "r1", "m", "m2", "r2", "s", "rows", "tps", "nq", "nt", "mx", "sub", "exp",
            "sum", "rs", "pad", "ptps", "pt"]}
        stats_loaded, tab_loaded, zrow_stored = sem("stats_loaded"), sem("tab_loaded"), sem("zrow_stored")
        tab_act, lin_chain, lin_ready = sem("tab_act"), sem("lin_chain"), sem("lin_ready")
        w3_zeroed = sem("w3_zeroed")
        cur_ready, mats_ready = sem("cur_ready"), sem("mats_ready")
        k1_ps, k1_ready, k2_ps, k2_ready, k3_ps, k3_ready = (sem(n) for n in (
            "k1_ps", "k1_ready", "k2_ps", "k2_ready", "k3_ps", "k3_ready"))
        xr_loaded = [sem("xr_loaded0"), sem("xr_loaded1")]
        xd_loaded = [sem("xd_loaded0"), sem("xd_loaded1")]
        t0_done, a_done, z1_done, t1_done, h1_done = (sem(n) for n in ("t0_done", "a_done", "z1_done", "t1_done", "h1_done"))
        b_done, t2_done, h2_done, c_done = (sem(n) for n in ("b_done", "t2_done", "h2_done", "c_done"))
        up_done, lo_done, sum_done, sgn_done, su_done, sl_done, sig_done, dif_done = (sem(n) for n in (
            "up_done", "lo_done", "sum_done", "sgn_done", "su_done", "sl_done", "sig_done", "dif_done"))
        lik_done, res_all = sem("lik_done"), sem("res_all")
        res_stored = [sem("res_stored0"), sem("res_stored1")]

        NW = 12
        block = ctx.enter_context(nc.Block())

        @block.sync
        def _(sp):
            for dst, src in ((wq_a[:, :], wqkv[0:CA, :]), (wq_b[:, :], wqkv[CA:C, :]), (dwc[:, :, :], wdw[:, :, :]),
                             (grp_a[:, :], grp[0:CA, :]), (grp_b[:, :], grp[CA:C, :]), (wp[:, :, :], wproj[:, :, :]),
                             (tmp_bc[:, :], temp[:, :]), (ident[:, :], ident_in[:, :]), (diag[:, :], diag_in[:, :])):
                sp.dma_start(dst, src).then_inc(w_loaded, 16)

            with sp.Fori(0, NB) as b:
                row0 = sp.snap(b * C)
                with sp.Fori(0, NBLK // 2) as j:
                    n8 = sp.snap(b * (NBLK // 2) + j)
                    for s in range(2):
                        col = sp.snap(j * (2 * BLK) + s * BLK)
                        sp.wait_ge(ya_done, b * NBLK)
                        sp.wait_ge(yb_done, b * NBLK)
                        sp.wait_ge(st_done[s], n8)
                        sp.dma_start(xa[:, s, :], x[bass.ds(row0, CA), bass.ds(col, BLK)]).then_inc(x_loaded[s], 16)
                        sp.dma_start(xb[:, s, :], x[bass.ds(row0 + CA, CB), bass.ds(col, BLK)]).then_inc(x_loaded[s], 16)
                sp.dma_start(xra[:, :], x[bass.ds(row0, CA), 0:W]).then_inc(row_loaded, 16)
                sp.dma_start(xrb[:, :], x[bass.ds(row0 + CA, CB), 0:W]).then_inc(row_loaded, 16)

                def conv_load(j, s, rows, st_all):
                    col = sp.snap(j * (2 * BLK) + (s * BLK + W)) if not isinstance(j, int) else (2 * j + s) * BLK + W
                    if st_all:
                        sp.wait_ge(st_done[s], (b + 1) * (NBLK // 2))
                    else:
                        sp.wait_ge(c1_ready, b * 81 + j * 10 + (5 * s - 4))
                    n = rows * W
                    c = bass.ds(col, n) if not isinstance(j, int) else slice(col, col + n)
                    sp.dma_start(xa[:, s, 0:n], x[bass.ds(row0, CA), c]).then_inc(x_loaded[s], 16)
                    sp.dma_start(xb[:, s, 0:n], x[bass.ds(row0 + CA, CB), c]).then_inc(x_loaded[s], 16)

                def conv_store(j, s):
                    static = isinstance(j, int)
                    col = (2 * j + s) * BLK if static else sp.snap(j * (2 * BLK) + s * BLK)
                    n8 = b * (NBLK // 2) + j
                    c = slice(col, col + BLK) if static else bass.ds(col, BLK)
                    sp.wait_ge(dw_chain, (b * NBLK + j * 2 + (s + 1)) * (NT * 8))
                    sp.dma_start(v_dram[bass.ds(b, 1), 0:CA, c].rearrange("a p n -> (a p) n"),
                                 acc[:, s, 3, :]).then_inc(v_stored[s], 16)
                    sp.wait_ge(t4_evac[s], n8 + 1)
                    for h in range(2):
                        dst = v_dram[bass.ds(b, 1), CA:C, c].rearrange("a p (r t w) -> (a p) r t w", t=2, w=W)[:, :, h, :]
                        sp.dma_start(dst, acc4[64 * h:64 * h + 64, s, :].rearrange("p (r w) -> p r w", w=W)
                                     ).then_inc(v4_stored[s], 16)

                conv_load(0, 0, RB, True)
                conv_load(0, 1, RB, True)
                with sp.Fori(1, NBLK // 2 - 1) as j:
                    for s in range(2):
                        conv_load(j, s, RB, False)
                        conv_store(j - 1, s)
                J = NBLK // 2 - 1
                conv_load(J, 0, RB, False)
                conv_store(J - 1, 0)
                conv_load(J, 1, RB - 1, False)
                conv_store(J - 1, 1)
                conv_store(J, 0)
                conv_store(J, 1)

                def x1_store(j, s):
                    col = (2 * j + s) * BLK if isinstance(j, int) else sp.snap(j * (2 * BLK) + s * BLK)
                    n8 = b * (NBLK // 2) + j
                    sp.wait_ge(ya_done, b * NBLK + j * 2 + (s + 1))
                    sp.dma_start(x1_dram[bass.ds(row0, CA), bass.ds(col, BLK)], oa[:, s, :]).then_inc(x1_stored[s], 16)
                    sp.wait_ge(yb_done, b * NBLK + j * 2 + (s + 1))
                    sp.dma_start(x1_dram[bass.ds(row0 + CA, CB), bass.ds(col, BLK)], ob[:, s, :]).then_inc(x1_stored[s], 16)

                sp.wait_ge(c1_ready, b * 81 + 81)
                for s in range(2):
                    sp.wait_ge(v_stored[s], b * (8 * NBLK) + 8 * NBLK)
                    sp.wait_ge(v4_stored[s], b * (16 * NBLK) + 16 * NBLK)

                def proj_load(j, s):
                    static = isinstance(j, int)
                    col = (2 * j + s) * BLK if static else sp.snap(j * (2 * BLK) + s * BLK)
                    n8 = b * (NBLK // 2) + j
                    if not static:
                        sp.wait_ge(ya_done, b * NBLK + j * 2 + (s - 1))
                        sp.wait_ge(yb_done, b * NBLK + j * 2 + (s - 1))
                    sp.dma_start(xa[:, s, :], x[bass.ds(row0, CA), bass.ds(col, BLK)]).then_inc(x_loaded[s], 16)
                    sp.dma_start(xb[:, s, :], x[bass.ds(row0 + CA, CB), bass.ds(col, BLK)]).then_inc(x_loaded[s], 16)
                    sp.dma_start(va[:, s, :], v_dram[bass.ds(b, 1), 0:CA, bass.ds(col, BLK)].rearrange("a p n -> (a p) n")).then_inc(v_loaded[s], 16)
                    sp.dma_start(vb[:, s, :], v_dram[bass.ds(b, 1), CA:C, bass.ds(col, BLK)].rearrange("a p n -> (a p) n")).then_inc(v_loaded[s], 16)

                proj_load(0, 0)
                proj_load(0, 1)
                with sp.Fori(1, NBLK // 2) as j:
                    for s in range(2):
                        x1_store(j - 1, s)
                        proj_load(j, s)
                for s in range(2):
                    x1_store(NBLK // 2 - 1, s)

            for s in range(2):
                sp.wait_ge(x1_stored[s], NB * 32 * NBLK // 2)
            sp.wait_ge(stat_stored, 32 * NB)
            sp.wait_ge(zrow_stored, 16)
            sp.wait_ge(gy["rstd_ready"], NB)
            sp.dma_start(tab[:, :, :], par[:, :, :]).then_inc(tab_loaded, 16)
            for f in range(3):
                sp.dma_start(sta[f * G:f * G + G, :, :], st_dram.rearrange("(i g) s -> g i s", g=G)).then_inc(stats_loaded, 16)

            def group(gi, rows):
                row = sp.snap(gi * G) if not isinstance(gi, int) else gi * G

                def rsel(ap, cols):
                    return ap[bass.ds(row, rows), cols] if not isinstance(row, int) else ap[row:row + rows, cols]

                def load_xr(it, s, chunks=3):
                    dyn = not isinstance(it, int)
                    col = sp.snap(it * TW) if dyn else it * TW
                    if not (isinstance(it, int) and it < 2):
                        sp.wait_ge(z1_done, gi * NU + 2 * it - 2)
                    sl = bass.ds(col, chunks * HALF) if dyn else slice(col, col + chunks * HALF)
                    for f in range(3):
                        sp.dma_start(xr[f * G:f * G + rows, s, 0:chunks * HALF], rsel(x1_dram, sl)).then_inc(xr_loaded[s], 16)

                def load_xd(it, s, chunks=3):
                    dyn = not isinstance(it, int)
                    cc = [sp.snap(it * TW + c * HALF) if dyn else it * TW + c * HALF for c in range(chunks)]
                    if not (isinstance(it, int) and it < 2):
                        sp.wait_ge(res_all, gi * NIT + it - 1)
                    for c in range(3):
                        c0 = cc[min(c, chunks - 1)]
                        sl = bass.ds(c0, HALF) if dyn else slice(c0, c0 + HALF)
                        sp.dma_start(xd[c * G:c * G + rows, s, :], rsel(x1_dram, sl)).then_inc(xd_loaded[s], 16)

                def store(it, s, chunks=3):
                    dyn = not isinstance(it, int)
                    cc = [sp.snap(it * TW + c * HALF) if dyn else it * TW + c * HALF for c in range(chunks)]
                    sp.wait_ge(res_all, gi * NIT + it + 1)
                    for c in range(chunks):
                        sl = bass.ds(cc[c], HALF) if dyn else slice(cc[c], cc[c] + HALF)
                        sp.dma_start(rsel(out, sl), res[c * G:c * G + rows, s, :]).then_inc(res_stored[s], 16)

                sp.wait_ge(res_all, gi * NIT)
                for it in range(2):
                    load_xr(it, it)
                    load_xd(it, it)
                for it in range(2, 4):
                    load_xr(it, it % 2)

                def turn(it, s):
                    store(it - 2, s)
                    load_xd(it, s)
                    load_xr(it + 2, s)

                with sp.Fori(1, 4) as p:
                    turn(2 * p, 0)
                    turn(2 * p + 1, 1)
                store(NIT - 5, 0)
                load_xd(NIT - 3, 0)
                load_xr(NIT - 1, 0, LASTC)
                store(NIT - 4, 1)
                load_xd(NIT - 2, 1)
                store(NIT - 3, 0)
                load_xd(NIT - 1, 0, LASTC)
                store(NIT - 2, 1)
                store(NIT - 1, 0, LASTC)

            with sp.Fori(0, NG - 1) as gi:
                group(gi, G)
            group(NG - 1, GLAST)
            sp.wait_ge(res_stored[0], NG * 16 * (5 * 3 + LASTC))
            sp.wait_ge(res_stored[1], NG * 16 * 15)
            sp.drain()

        @block.gpsimd
        def _(pool):
            nc.gpsimd.memset(zt[:, :], 0.0).then_inc(zeroed, 1)
            nc.gpsimd.memset(pbuf[:, :, :, :, :], 0.0)
            nc.gpsimd.memset(p4[:, :, :, :], 0.0)
            nc.gpsimd.memset(mv[:, :, :], 0.0)
            nc.gpsimd.memset(apad[:, :, :], 0.0)
            nc.gpsimd.memset(band[:, :, :], 0.0).then_inc(zeroed, 1)
            pool.wait_ge(zeroed, 1)
            pool.dma_start(st_dram[ROWS:NG * G, :], zt[0:NG * G - ROWS, 0:2]).then_inc(zrow_stored, 16)

            def fin(gi, it):
                n = gi * NIT + it
                pool.wait_ge(up_done, n + 1)
                pool.wait_ge(lo_done, n + 1)
                pool.wait_ge(sgn_done, n)
                nc.gpsimd.tensor_tensor(ssum[:, :], lo_c[:, :], up_c[:, :], ALU.add).then_inc(sum_done, 1)
                pool.wait_ge(sgn_done, n + 1)
                pool.wait_ge(sig_done, n)
                nc.gpsimd.tensor_tensor(sul[:, 1, :], up_c[:, :], sgn[:, :], ALU.mult).then_inc(su_done, 1)
                pool.wait_ge(sig_done, n + 1)
                pool.wait_ge(lik_done, n)
                nc.gpsimd.tensor_tensor(dif[:, :], sig[:, 1, :], sig[:, 0, :], ALU.subtract).then_inc(dif_done, 1)

            with pool.Fori(0, NG) as gi:
                with pool.Fori(0, NIT) as it:
                    fin(gi, it)

        @block.scalar
        def _(act):
            act.wait_ge(zeroed, 2)

            with act.Fori(0, NB) as b:
                b1 = act.snap(b + 1)

                def group_sqrt(g):
                    act.wait_ge(g["ve_ready"], b1)
                    nc.scalar.activation(gs[:, 4, :], gs[:, 3, :], ACT.Sqrt).then_inc(g["sd_ready"], 1)

                group_sqrt(gx)
                act.wait_ge(bias_ps, b1)
                nc.scalar.activation(bias[:, :], ps[:, T4O, 4:9], ACT.Identity).then_inc(bias_ready, 1)
                act.wait_ge(bias_ready, b1)
                nc.scalar.activation(pbuf[:, 0, :, 0, :], zt[:, :].rearrange("p (t w) -> p t w", w=PW), ACT.Copy)
                nc.scalar.activation(p4[0:64, 0, 0, :], zt[0:64, 0:PW], ACT.Copy)
                act.wait_ge(c1_ready, b * 81 + 1)
                for t in range(NT):
                    nc.scalar.activation(pbuf[:, 0, t, 1, 1:1 + W], ps[:, 0, t * W:t * W + W], ACT.Identity, bias=bias[:, t:t + 1])
                nc.scalar.activation(p4[64:128, 0, 0, 1:1 + W], ps[64:128, 1, 0:W], ACT.Identity,
                                     bias=bias[64:128, 4:5]).then_inc(evac_done, 1)

                def step(j, s, first, last):
                    n8 = b * (NBLK // 2) + j
                    seq = b * 81 + j * 10 + (5 * s + 1)
                    if not isinstance(j, int) or j > 0:
                        act.wait_ge(dw_chain, (b * NBLK + j * 2 + (s - 1)) * (NT * 8))
                    act.wait_ge(t4_done[s], n8)
                    if not first:
                        act.wait_ge(evac_done, seq)
                        nc.scalar.activation(pbuf[:, s, :, 0:2, :], pbuf[:, 1 - s, :, RB:RB + 2, :].rearrange("p t r w -> p t r w"), ACT.Copy)
                        nc.scalar.activation(p4[:, s, 0, :], p4[:, 1 - s, RB // 2, :], ACT.Copy)
                    if last:
                        nc.scalar.activation(pbuf[:, s, :, RB + 1, :], zt[:, :].rearrange("p (t w) -> p t w", w=PW), ACT.Copy)
                        nc.scalar.activation(p4[64:128, s, RB // 2, :], zt[64:128, 0:PW], ACT.Copy)
                    rows = RB - 1 if last else RB
                    for k in range(5):
                        cs = (1 + s + k) % 2
                        src = c1set(cs).rearrange("p a (r w) -> p (a r) w", w=W)
                        act.wait_ge(c1_ready, seq + k + 1)
                        if k == 0:
                            nh = RB // 2 - 1 if last else RB // 2
                            nc.scalar.activation(p4[0:64, s, 1:, 1:1 + W], src[0:64, 0:RB:2, :], ACT.Identity, bias=bias[0:64, 4:5])
                            nc.scalar.activation(p4[64:128, s, 1:1 + nh, 1:1 + W], src[64:128, 1:2 * nh:2, :], ACT.Identity,
                                                 bias=bias[64:128, 4:5]).then_inc(evac_done, 1)
                        else:
                            t = k - 1
                            nc.scalar.activation(pbuf[:, s, t, 2:2 + rows, 1:1 + W], src[:, 0:rows, :], ACT.Identity,
                                                 bias=bias[:, t:t + 1]).then_inc(evac_done, 1)
                            if t == 0:
                                act.wait_ge(tr_done[s], n8 * 8)
                            if t == 3:
                                act.wait_ge(v_stored[s], n8 * 16)
                            act.wait_ge(evac_done, seq + k + 1)
                            nc.scalar.activation(acc[:, s, t, :].rearrange("p (r w) -> p r w", w=W),
                                                 pbuf[:, s, t, 1:1 + RB, 1:1 + W], ACT.Copy, scale=dwc[:, t, 4:5]).then_inc(tap_done, 1)
                    act.wait_ge(t4_done[s], n8 + 1)
                    act.wait_ge(v4_stored[s], n8 * 32)
                    nc.scalar.activation(acc4[:, s, :], ps[:, T4O, :], ACT.Copy).then_inc(t4_evac[s], 1)

                def evac_transposed(j, s, first):
                    base = b * 128 + j * 16 + 8 * s
                    for c in range(8):
                        act.wait_ge(tr_done[s], (b * (NBLK // 2) + j) * 8 + c + 1)
                        if not (first and c < 2):
                            act.wait_ge(gr_done, base + c - 1)
                        nc.scalar.activation(qkt[:, c % 2, :], ps[:, TR + c % 2, 0:384], ACT.Copy).then_inc(tr_evac, 1)

                step(0, 0, True, False)
                step(0, 1, False, False)
                evac_transposed(0, 0, True)
                with act.Fori(1, NBLK // 2 - 1) as j:
                    step(j, 0, False, False)
                    evac_transposed(j - 1, 1, False)
                    step(j, 1, False, False)
                    evac_transposed(j, 0, False)
                J = NBLK // 2 - 1
                step(J, 0, False, False)
                evac_transposed(J - 1, 1, False)
                step(J, 1, False, True)
                evac_transposed(J, 0, False)
                evac_transposed(J, 1, False)

                act.wait_ge(A["n2"], b1)
                nc.scalar.activation(nrm[:, 1, :], nrm[:, 0, :], ACT.Sqrt).then_inc(A["n"], 1)
                act.wait_ge(A["sub"], b1)
                nc.scalar.activation(at[:, 2, :, :], at[:, 1, :, :], ACT.Exp).then_inc(A["exp"], 1)
                group_sqrt(gy)
                act.wait_ge(gy["rstd_ready"], b1)
                for n, r0, rn in ((0, 0, CA), (1, CA, CB)):
                    act.dma_start(st_dram[bass.ds(b * C + r0, rn), :], gs[0:rn, 6, :] if n == 0 else gs[0:rn, 7, :]
                                  ).then_inc(stat_stored, 16)

            act.wait_ge(tab_loaded, 16)
            nc.scalar.activation(tab[:, :, 8:11], tab[:, :, 8:11], ACT.Tanh)
            nc.scalar.activation(sp_e[:, :, :], tab[:, :, 0:8], ACT.Abs).then_inc(tab_act, 1)
            act.wait_ge(tab_act, 1)
            nc.scalar.activation(sp_e[:, :, :], sp_e[:, :, :], ACT.Exp, scale=-1.0).then_inc(tab_act, 1)
            act.wait_ge(lin_chain, 1)
            nc.scalar.activation(sp_l[:, :, :], sp_u[:, :, :], ACT.Ln).then_inc(tab_act, 1)

            def t0(gi, it, side, par, chunks):
                u = gi * NU + 2 * it + side
                if side == 0:
                    if isinstance(it, int):
                        act.wait_ge(xr_loaded[par], gi * (48 * (6 - par)) + 48 * (it // 2 + 1))
                    else:
                        act.wait_ge(xr_loaded[par], gi * (48 * (6 - par)) + (it - par) * 24 + 48)
                if not (isinstance(it, int) and it == 0):
                    act.wait_ge(a_done, u - 1)
                n = chunks * HALF
                nc.scalar.activation(t0b[:, side, 0:n], xr[:, par, 0:n], ACT.Tanh, scale=cur[:, 0:1],
                                     bias=cur[:, 1 + side:2 + side]).then_inc(t0_done, 1)

            def t1(gi, it, side, chunks):
                u = gi * NU + 2 * it + side
                act.wait_ge(z1_done, u + 1)
                if not (isinstance(it, int) and it == 0):
                    act.wait_ge(h2_done, u - 1)
                n = chunks * HALF
                nc.scalar.activation(t12[:, side, 0:n], zb[:, side, 0:n], ACT.Tanh,
                                     bias=cst[:, 1 + side:2 + side]).then_inc(t1_done, 1)

            def t2(gi, it, side, chunks):
                u = gi * NU + 2 * it + side
                act.wait_ge(b_done, u + 1)
                n = chunks * HALF
                nc.scalar.activation(t12[:, side, 0:n].rearrange("p (a n) -> p a n", n=HALF), ps[:, PB:PB + chunks, :][0:GP],
                                     ACT.Tanh, bias=cst[:, 3 + side:4 + side]).then_inc(t2_done, 1)

            def fin_up(gi, it):
                n = gi * NIT + it
                act.wait_ge(c_done, gi * NU + 2 * it + 2)
                act.wait_ge(su_done, n)
                nc.scalar.activation(up_c[:, :], ps[0:GP, PC + 1, :], ACT.Identity, bias=cst[:, 6:7]).then_inc(up_done, 1)

            def fin_sign(gi, it):
                n = gi * NIT + it
                act.wait_ge(sum_done, n + 1)
                act.wait_ge(sl_done, n)
                act.wait_ge(su_done, n)
                nc.scalar.activation(sgn[:, :], ssum[:, :], ACT.Sign).then_inc(sgn_done, 1)

            def fin_sigmoid(gi, it):
                n = gi * NIT + it
                act.wait_ge(su_done, n + 1)
                act.wait_ge(sl_done, n + 1)
                act.wait_ge(dif_done, n)
                nc.scalar.activation(sig[:, :, :], sul[:, :, :], ACT.Sigmoid, scale=-1.0).then_inc(sig_done, 1)

            def fin_abs(gi, it):
                n = gi * NIT + it
                act.wait_ge(dif_done, n + 1)
                act.wait_ge(res_all, n)
                nc.scalar.activation(lik[:, :], dif[:, :], ACT.Abs).then_inc(lik_done, 1)

            def body(gi, it, par):
                ch = chunks_of(it)
                if has(it):
                    t0(gi, it, 1, par, ch)
                if has(it - 2):
                    fin_up(gi, it - 2)
                if has(it):
                    t1(gi, it, 0, ch)
                if has(it - 2):
                    fin_sign(gi, it - 2)
                if has(it - 1):
                    t2(gi, it - 1, 1, chunks_of(it - 1))
                if has(it + 1):
                    t0(gi, it + 1, 0, 1 - par, chunks_of(it + 1))
                if has(it - 2):
                    fin_sigmoid(gi, it - 2)
                if has(it):
                    t1(gi, it, 1, ch)
                if has(it - 2):
                    fin_abs(gi, it - 2)
                if has(it):
                    t2(gi, it, 0, ch)

            def group(gi):
                act.wait_ge(k3_ready, gi + 1)
                t0(gi, 0, 0, 0, 3)
                body(gi, 0, 0)
                body(gi, 1, 1)
                with act.Fori(1, 5) as p:
                    body(gi, 2 * p, 0)
                    body(gi, 2 * p + 1, 1)
                body(gi, 10, 0)
                body(gi, 11, 1)
                body(gi, 12, 0)

            with act.Fori(0, NG) as gi:
                group(gi)

        @block.tensor
        def _(pe):
            pe.wait_ge(w_loaded, 16 * 9)
            pe.wait_ge(band_ready, 1)

            def mm(o, l, r, start=True, stop=True, **kw):
                return nc.tensor.matmul(o, l, r, start=start, stop=stop, **kw)

            with pe.Fori(0, NB) as b:
                b1 = pe.snap(b + 1)

                def group_means(g, src, col, ready, done):
                    pe.wait_ge(g[ready], b1)
                    for t in range(2):
                        mm(ps[:, T4O, col + t:col + t + 1], grp_a[:, t * 128:t * 128 + 128], src[:, 0:1], stop=False)
                        last = mm(ps[:, T4O, col + t:col + t + 1], grp_b[:, t * 128:t * 128 + 128], src[0:CB, 1:2], start=False)
                    last.then_inc(g[done], 1)

                group_means(gx, mv[:, :, 0], 0, "mv_ready", "mg_ready")
                group_means(gx, gs[:, 2, :], 2, "q_ready", "vg_ready")
                pe.wait_ge(ws_ready, b1)
                for t in range(5):
                    mm(ps[:, T4O, 4 + t:5 + t], ws_a[:, t * 128:t * 128 + 128], gs[:, 5, 0:1], stop=False)
                    last = mm(ps[:, T4O, 4 + t:5 + t], ws_b[:, t * 128:t * 128 + 128], gs[0:CB, 5, 1:2], start=False)
                last.then_inc(bias_ps, 1)
                mm(ps[0:96, GR, 0:384], zt[:, 0:96], zt[:, 0:384])
                pe.wait_ge(row_loaded, b1 * 32)
                for t in range(5):
                    o = ps[:, 0, t * W:t * W + W] if t < NT else ps[:, 1, 0:W]
                    mm(o, ws_a[:, t * 128:t * 128 + 128], xra[:, :], stop=False)
                    last = mm(o, ws_b[:, t * 128:t * 128 + 128], xrb[:, :], start=False)
                last.then_inc(c1_ready, 1)

                def conv1x1(j, s):
                    n8 = b * (NBLK // 2) + j
                    seq = b * 81 + j * 10 + (5 * s + 1)
                    pe.wait_ge(x_loaded[s], b * (32 * 24) + j * 32 + 32 * 9)
                    for k in range(5):
                        t = 4 if k == 0 else k - 1
                        cs = (1 + s + k) % 2
                        pe.wait_ge(evac_done, seq + k - 1)
                        for h in range(2):
                            o = ps[:, 2 * cs + h, :]
                            mm(o, ws_a[:, t * 128:t * 128 + 128], xa[:, s, h * HALF:h * HALF + HALF], stop=False)
                            last = mm(o, ws_b[:, t * 128:t * 128 + 128], xb[:, s, h * HALF:h * HALF + HALF], start=False)
                        last.then_inc(c1_ready, 1)

                def conv_tile4(j, s):
                    n8 = b * (NBLK // 2) + j
                    seq = b * 81 + j * 10 + (5 * s + 1)
                    pe.wait_ge(evac_done, seq + 1)
                    if s == 0:
                        pe.wait_ge(t4_evac[1], n8)
                    else:
                        pe.wait_ge(t4_evac[0], n8 + 1)
                    for k in range(6):
                        dx, blk = k % 3, k // 3
                        last = mm(ps[:, T4O, :], band[:, k, :], p4[:, s, blk:blk + RB // 2, dx:dx + W], start=k == 0, stop=k == 5)
                    last.then_inc(t4_done[s], 1)

                def transposes(j, s, c, first):
                    nt = (b * (NBLK // 2) + j)
                    base = b * 128 + j * 16 + 8 * s
                    if c == 0:
                        pe.wait_ge(dw_chain, (b * NBLK + j * 2 + (s + 1)) * (NT * 8) - 1)
                    if not (first and c < 2):
                        pe.wait_ge(tr_evac, base + c - 1)
                    for t in range(3):
                        last = nc.tensor.transpose(ps[:, TR + c % 2, t * 128:t * 128 + 128],
                                                   acc[:, s, t, c * 128:c * 128 + 128], ident[:, :])
                    last.then_inc(tr_done[s], 1)

                def gram_mm(j, s, c):
                    base = b * 128 + j * 16 + 8 * s
                    pe.wait_ge(tr_evac, base + c + 1)
                    for h in range(HEADS):
                        qk = qkt[:, c % 2, h * 96:h * 96 + 96]
                        last = mm(ps[0:96, GR, h * 96:h * 96 + 96], qk, qk, start=False, stop=False, skip_group_check=True)
                    last.then_inc(gr_done, 1)

                def tg(j, s, first):
                    transposes(j, s, 0, first)
                    for c in range(1, 8):
                        transposes(j, s, c, first)
                        gram_mm(j, s, c - 1)
                    gram_mm(j, s, 7)

                def step(j, s):
                    conv1x1(j, s)
                    conv_tile4(j, s)

                step(0, 0)
                step(0, 1)
                tg(0, 0, True)
                with pe.Fori(1, NBLK // 2) as j:
                    step(j, 0)
                    tg(j - 1, 1, False)
                    step(j, 1)
                    tg(j, 0, False)
                tg(NBLK // 2 - 1, 1, False)

                pe.wait_ge(A["rows"], b1)
                for h in range(HEADS):
                    last = nc.tensor.transpose(ps[0:96, TR, h * 96:h * 96 + 96], gtmp[:, h, :], ident[0:96, 0:96])
                last.then_inc(A["tps"], 1)
                pe.wait_ge(A["pad"], b1)
                for h in range(HEADS):
                    mm(ps[:, TR + 1, 0:C], apad[:, h, 0:CA], wp[:, h, :], start=h == 0, stop=h == HEADS - 1)
                for h in range(HEADS):
                    last = mm(ps[0:CB, TR, 0:C], apad[:, h, CA:C], wp[:, h, :], start=h == 0, stop=h == HEADS - 1)
                last.then_inc(A["ptps"], 1)

                with pe.Fori(0, NBLK // 2) as j:
                    for s in range(2):
                        n16 = b * NBLK + j * 2 + s
                        pe.wait_ge(v_loaded[s], (b * (NBLK // 2) + j) * 32 + 32)
                        pe.wait_ge(A["pt"], b1)
                        pe.wait_ge(ya_done, n16)
                        for h in range(2):
                            mm(ps[:, h, :], pt_a[:, 0:CA], va[:, s, h * HALF:h * HALF + HALF], stop=False)
                            last = mm(ps[:, h, :], pt_b[:, 0:CA], vb[:, s, h * HALF:h * HALF + HALF], start=False)
                        last.then_inc(ya_ready, 1)
                        pe.wait_ge(yb_done, n16)
                        for h in range(2):
                            mm(ps[0:CB, 2 + h, :], pt_a[:, CA:C], va[:, s, h * HALF:h * HALF + HALF], stop=False)
                            last = mm(ps[0:CB, 2 + h, :], pt_b[:, CA:C], vb[:, s, h * HALF:h * HALF + HALF], start=False)
                        last.then_inc(yb_ready, 1)
                group_means(gy, mv[:, :, 0], 0, "mv_ready", "mg_ready")
                group_means(gy, gs[:, 2, :], 2, "q_ready", "vg_ready")

            def stage_a(gi, it, side, ch):
                u = gi * NU + 2 * it + side
                pe.wait_ge(t0_done, u + 1)
                pe.wait_ge(z1_done, u)
                for c in range(ch):
                    last = mm(ps[0:GP, PA + c, :], w1[:, :], t0b[:, side, c * HALF:c * HALF + HALF])
                last.then_inc(a_done, 1)

            def stage_b(gi, it, side, ch):
                u = gi * NU + 2 * it + side
                pe.wait_ge(h1_done, u + 1)
                pe.wait_ge(h2_done, u)
                for c in range(ch):
                    last = mm(ps[0:GP, PB + c, :], w2[:, :], zb[:, side, c * HALF:c * HALF + HALF])
                last.then_inc(b_done, 1)

            def stage_c(gi, it, side, ch):
                u = gi * NU + 2 * it + side
                pe.wait_ge(h2_done, u + 1)
                pe.wait_ge(up_done if side else lo_done, gi * NIT + it)
                for c in range(ch):
                    last = mm(ps[0:GP, PC + side, :], w3[:, c, :], hb[:, side, c * HALF:c * HALF + HALF], start=c == 0, stop=c == ch - 1)
                last.then_inc(c_done, 1)

            def body(gi, it):
                ch = chunks_of(it)
                if has(it):
                    stage_a(gi, it, 0, ch)
                if has(it - 1):
                    stage_b(gi, it - 1, 1, chunks_of(it - 1))
                    stage_c(gi, it - 1, 0, chunks_of(it - 1))
                if has(it):
                    stage_a(gi, it, 1, ch)
                    stage_b(gi, it, 0, ch)
                if has(it - 1):
                    stage_c(gi, it - 1, 1, chunks_of(it - 1))

            with pe.Fori(0, NG) as gi:
                pe.wait_ge(mats_ready, gi + 1)
                mm(ps[0:GP, PA, 0:3], bd1[:, :], cur[:, 0:3]).then_inc(k1_ps, 1)
                pe.wait_ge(k1_ready, gi + 1)
                mm(ps[0:GP, PA + 1, 0:2], w2[:, :], cst[:, 1:3]).then_inc(k2_ps, 1)
                pe.wait_ge(k2_ready, gi + 1)
                mm(ps[0:GP, PA + 2, 0:2], w3[:, 3, :], cst[:, 3:5]).then_inc(k3_ps, 1)
                pe.wait_ge(k3_ready, gi + 1)
                body(gi, 0)
                with pe.Fori(1, 10) as it:
                    body(gi, it)
                body(gi, 10)
                body(gi, 11)

        @block.vector
        def _(dve):
            dve.wait_ge(w_loaded, 16 * 9)
            dve.wait_ge(zeroed, 2)
            for k in range(6):
                dx, blk = k % 3, k // 3
                for h in range(2):
                    for ho in range(2):
                        dy = 2 * blk + h - ho
                        if 0 <= dy < 3:
                            last = nc.vector.tensor_scalar(band[64 * h:64 * h + 64, k, 64 * ho:64 * ho + 64],
                                                           ident[64 * h:64 * h + 64, 64 * h:64 * h + 64],
                                                           dwc[64 * h:64 * h + 64, 4, 3 * dy + dx:3 * dy + dx + 1], None, ALU.mult)
            last.then_inc(band_ready, 1)

            with dve.Fori(0, NB) as b:
                b1 = dve.snap(b + 1)

                def group_stats(g, start_wait):
                    start_wait()
                    nc.vector.memset(gs[:, 0, 0:1], 0.0).then_inc(g["mv_marked"], 1)
                    nc.vector.bn_aggr(mv[:, 0, :], bs_a[:, :, :].rearrange("p a s -> p (a s)"))
                    nc.vector.bn_aggr(mv[0:CB, 1, :], bs_b[:, :, :].rearrange("p a s -> p (a s)")).then_inc(g["mv_ready"], 1)
                    dve.wait_ge(g["mg_ready"], b1)
                    nc.vector.tensor_tensor(gs[:, 0, :], mv[:, :, 0], ps[:, T4O, 0:2], ALU.subtract)
                    nc.vector.tensor_scalar(gs[:, 5, :], ps[:, T4O, 0:2], -1.0, None, ALU.mult).then_inc(g["dev_ready"], 1)
                    dve.wait_ge(g["dev_ready"], b1)
                    nc.vector.tensor_tensor(gs[:, 1, :], gs[:, 0, :], gs[:, 0, :], ALU.mult).then_inc(g["dsq_ready"], 1)
                    dve.wait_ge(g["dsq_ready"], b1)
                    nc.vector.tensor_tensor(gs[:, 2, :], gs[:, 1, :], mv[:, :, 1], ALU.add).then_inc(g["q_ready"], 1)
                    dve.wait_ge(g["vg_ready"], b1)
                    nc.vector.tensor_scalar(gs[:, 3, :], ps[:, T4O, 2:4], GN_EPS, None, ALU.add).then_inc(g["ve_ready"], 1)
                    dve.wait_ge(g["sd_ready"], b1)

                with dve.Fori(0, NBLK // 2) as j:
                    for s in range(2):
                        c0 = dve.snap(j * 4 + 2 * s)
                        c1 = dve.snap(j * 4 + 2 * s + 1)
                        dve.wait_ge(x_loaded[s], b * (32 * 24) + j * 32 + 32)
                        dve.wait_ge(zeroed, 2)
                        for h, c in ((0, c0), (1, c1)):
                            nc.vector.bn_stats(bs_a[:, bass.ds(c, 1), :].rearrange("p a s -> p (a s)"), xa[:, s, h * HALF:h * HALF + HALF])
                            last = nc.vector.bn_stats(bs_b[:, bass.ds(c, 1), :].rearrange("p a s -> p (a s)"), xb[:, s, h * HALF:h * HALF + HALF])
                        last.then_inc(st_done[s], 1)

                def x_waits():
                    dve.wait_ge(st_done[0], b1 * (NBLK // 2))
                    dve.wait_ge(st_done[1], b1 * (NBLK // 2))
                group_stats(gx, x_waits)
                nc.vector.reciprocal(gs[:, 1, :], gs[:, 4, :]).then_inc(gx["rstd_ready"], 1)
                dve.wait_ge(gx["rstd_ready"], b1)
                nc.vector.tensor_scalar(ws_a[:, :], wq_a[:, :], gs[:, 1, 0:1], None, ALU.mult)
                nc.vector.tensor_scalar(ws_b[:, :], wq_b[:, :], gs[0:CB, 1, 1:2], None, ALU.mult).then_inc(ws_ready, 1)

                def conv(j, s):
                    n8 = b * (NBLK // 2) + j
                    tb = b * (NBLK * NT) + j * (2 * NT) + NT * s
                    chain = (b * NBLK + j * 2 + s) * (NT * 8)
                    k = 0
                    for pair in ((0, 1), (2, 3)):
                        for n, tap in enumerate(TAPS):
                            dy, dx = tap // 3, tap % 3
                            for t in pair:
                                if n == 0:
                                    dve.wait_ge(tap_done, tb + t + 1)
                                else:
                                    dve.wait_ge(dw_chain, chain + k - 1)
                                a = acc[:, s, t, :].rearrange("p (r w) -> p r w", w=W)
                                i = nc.vector.scalar_tensor_tensor(out=a, in0=pbuf[:, s, t, dy:dy + RB, dx:dx + W],
                                                                   scalar=dwc[:, t, tap:tap + 1], in1=a, op0=ALU.mult, op1=ALU.add)
                                i.then_inc(dw_chain, 1)
                                k += 1

                with dve.Fori(0, NBLK // 2) as j:
                    conv(j, 0)
                    conv(j, 1)

                def then(i, name):
                    i.then_inc(A[name], 1)
                    dve.wait_ge(A[name], b1)

                dve.wait_ge(gr_done, b1 * 128)
                then(nc.vector.tensor_copy(gram[:, :, :].rearrange("p h d -> p (h d)"), ps[0:96, GR, 0:384]), "gram")
                for h in range(HEADS):
                    last = nc.vector.tensor_tensor(gtmp[:, h, :], gram[:, h, :], ident[0:96, 0:96], ALU.mult)
                then(last, "diag")
                last = nc.vector.tensor_reduce(nrm[:, 0, :], gtmp[:, :, :], AX.X, ALU.add)
                last.then_inc(A["n2"], 1)
                dve.wait_ge(A["n"], b1)
                then(nc.vector.tensor_scalar(nrm[:, 2, :], nrm[:, 1, :], EPS, None, ALU.add), "ne")
                then(nc.vector.reciprocal(nrm[:, 3, :], nrm[:, 2, :]), "r1")
                then(nc.vector.tensor_tensor(nrm[:, 4, :], nrm[:, 1, :], nrm[:, 3, :], ALU.mult), "m")
                then(nc.vector.tensor_scalar(nrm[:, 5, :], nrm[:, 4, :], EPS, None, ALU.max), "m2")
                then(nc.vector.reciprocal(nrm[:, 6, :], nrm[:, 5, :]), "r2")
                then(nc.vector.tensor_tensor(nrm[:, 7, :], nrm[:, 3, :], nrm[:, 6, :], ALU.mult), "s")
                for h in range(HEADS):
                    last = nc.vector.tensor_scalar(gtmp[:, h, :], gram[:, h, :], nrm[:, 7, h:h + 1], None, ALU.mult)
                last.then_inc(A["rows"], 1)
                dve.wait_ge(A["tps"], b1)
                for h in range(HEADS):
                    last = nc.vector.tensor_scalar(at[:, 0, h, :], ps[0:CH, TR, h * 96 + CH:h * 96 + 96],
                                                   nrm[0:CH, 7, h:h + 1], tmp_bc[:, h:h + 1], ALU.mult, ALU.mult)
                then(last, "nq")
                then(nc.vector.tensor_reduce(nrm[0:CH, 0, :], at[:, 0, :, :], AX.X, ALU.max), "mx")
                for h in range(HEADS):
                    last = nc.vector.tensor_scalar(at[:, 1, h, :], at[:, 0, h, :], nrm[0:CH, 0, h:h + 1], None, ALU.subtract)
                last.then_inc(A["sub"], 1)
                dve.wait_ge(A["exp"], b1)
                then(nc.vector.tensor_reduce(nrm[0:CH, 1, :], at[:, 2, :, :], AX.X, ALU.add), "sum")
                then(nc.vector.reciprocal(nrm[0:CH, 2, :], nrm[0:CH, 1, :]), "rs")
                for h in range(HEADS):
                    last = nc.vector.tensor_scalar(apad[:, h, h * CH:h * CH + CH], at[:, 2, h, :], nrm[0:CH, 2, h:h + 1], None, ALU.mult)
                last.then_inc(A["pad"], 1)
                dve.wait_ge(A["ptps"], b1)
                nc.vector.tensor_copy(pt_a[:, :], ps[:, TR + 1, 0:C])
                nc.vector.tensor_copy(pt_b[:, :], ps[0:CB, TR, 0:C]).then_inc(A["pt"], 1)

                with dve.Fori(0, NBLK // 2) as j:
                    n8 = dve.snap(b * (NBLK // 2) + j)
                    for s in range(2):
                        c0 = dve.snap(j * 4 + 2 * s)
                        c1 = dve.snap(j * 4 + 2 * s + 1)
                        n16 = b * NBLK + j * 2 + s
                        dve.wait_ge(x_loaded[s], b * (32 * 24) + j * 32 + 32 * 17)
                        dve.wait_ge(x1_stored[s], n8 * 32)
                        dve.wait_ge(ya_ready, n16 + 1)
                        i = nc.vector.tensor_tensor(oa[:, s, :].rearrange("p (a n) -> p a n", a=2), xa[:, s, :].rearrange("p (a n) -> p a n", a=2),
                                                    ps[:, 0:2, :], ALU.add)
                        i.then_inc(ya_done, 1)
                        dve.wait_ge(yb_ready, n16 + 1)
                        i = nc.vector.tensor_tensor(ob[:, s, :].rearrange("p (a n) -> p a n", a=2), xb[:, s, :].rearrange("p (a n) -> p a n", a=2),
                                                    ps[0:CB, 2:4, :], ALU.add)
                        i.then_inc(yb_done, 1)
                        dve.wait_ge(ya_done, n16 + 1)
                        dve.wait_ge(yb_done, n16 + 1)
                        dve.wait_ge(zeroed, 2)
                        for h, c in ((0, c0), (1, c1)):
                            nc.vector.bn_stats(bs_a[:, bass.ds(c, 1), :].rearrange("p a s -> p (a s)"), oa[:, s, h * HALF:h * HALF + HALF])
                            last = nc.vector.bn_stats(bs_b[:, bass.ds(c, 1), :].rearrange("p a s -> p (a s)"), ob[:, s, h * HALF:h * HALF + HALF])
                        last.then_inc(y_stats, 1)

                def y_waits():
                    dve.wait_ge(y_stats, b1 * NBLK)
                group_stats(gy, y_waits)
                dve.wait_ge(stat_stored, b * 32)
                for t in range(2):
                    nc.vector.tensor_scalar(gs[:, 6 + t, 0:1], gs[:, 5, t:t + 1], -1.0, None, ALU.mult)
                    last = nc.vector.reciprocal(gs[:, 6 + t, 1:2], gs[:, 4, t:t + 1])
                last.then_inc(gy["rstd_ready"], 1)

            dve.wait_ge(tab_loaded, 16)
            nc.vector.memset(w3[:, :, :], 0.0).then_inc(w3_zeroed, 1)
            dve.wait_ge(stats_loaded, 48)
            dve.wait_ge(tab_act, 2)
            n = [0]

            def link(i):
                n[0] += 1
                i.then_inc(lin_chain, 1)
                dve.wait_ge(lin_chain, n[0])

            link(nc.vector.tensor_scalar(sp_u[:, :, :], sp_e[:, :, :], 1.0, None, ALU.add))
            dve.wait_ge(tab_act, 3)
            link(nc.vector.tensor_scalar(sp_u[:, :, :], sp_u[:, :, :], 1.0, None, ALU.subtract))
            link(nc.vector.tensor_scalar(sp_m[:, :, :], sp_u[:, :, :], 0.0, None, ALU.is_equal))
            link(nc.vector.tensor_tensor(sp_l[:, :, :], sp_l[:, :, :], sp_m[:, :, :], ALU.add))
            link(nc.vector.tensor_tensor(sp_u[:, :, :], sp_u[:, :, :], sp_m[:, :, :], ALU.add))
            link(nc.vector.reciprocal(sp_m[:, :, :], sp_u[:, :, :]))
            link(nc.vector.tensor_tensor(sp_l[:, :, :], sp_l[:, :, :], sp_m[:, :, :], ALU.mult))
            link(nc.vector.tensor_tensor(sp_l[:, :, :], sp_l[:, :, :], sp_e[:, :, :], ALU.mult))
            link(nc.vector.scalar_tensor_tensor(out=tab[:, :, 0:8], in0=tab[:, :, 0:8], scalar=0.0, in1=sp_l[:, :, :], op0=ALU.max, op1=ALU.add))
            link(nc.vector.tensor_tensor(lin[:, :, 0], tab[:, :, 0], sta[:, :, 1], ALU.mult))
            link(nc.vector.tensor_tensor(wrk[:, :, 0], lin[:, :, 0], sta[:, :, 0], ALU.mult))
            link(nc.vector.tensor_tensor(wrk[:, :, 1], tab[:, :, 11], wrk[:, :, 0], ALU.subtract))
            link(nc.vector.scalar_tensor_tensor(out=lin[:, :, 1], in0=tab[:, :, 0], scalar=-0.5, in1=wrk[:, :, 1], op0=ALU.mult, op1=ALU.add))
            link(nc.vector.scalar_tensor_tensor(out=lin[:, :, 2], in0=tab[:, :, 0], scalar=0.5, in1=wrk[:, :, 1], op0=ALU.mult, op1=ALU.add))
            for o in range(3):
                link(nc.vector.tensor_tensor(w1t[:, :, o], tab[:, :, 1 + o], tab[:, :, 8], ALU.mult))

            PARO = 6

            def prepare(gi):
                g0 = dve.snap(gi)
                dve.wait_ge(res_all, gi * NIT)
                dve.wait_ge(w3_zeroed, 1)
                nc.vector.tensor_copy(cur[:, 0:3], lin[:, bass.ds(g0, 1), :].rearrange("p a s -> p (a s)"))
                nc.vector.tensor_copy(cur[:, 3:6], w1t[:, bass.ds(g0, 1), :].rearrange("p a s -> p (a s)"))
                nc.vector.tensor_copy(cur[:, PARO:PARO + NPAR], tab[:, bass.ds(g0, 1), :].rearrange("p a s -> p (a s)")).then_inc(cur_ready, 1)
                dve.wait_ge(cur_ready, gi + 1)
                for o in range(3):
                    c = slice(o * G, o * G + G)
                    nc.vector.tensor_scalar(bd1[:, c], diag[:, :], cur[:, PARO + 1 + o:PARO + 2 + o], None, ALU.mult)
                    nc.vector.tensor_scalar(w1[:, c], diag[:, :], cur[:, 3 + o:4 + o], None, ALU.mult)
                    nc.vector.tensor_scalar(w2[:, c], diag[:, :], cur[:, PARO + 4 + o:PARO + 5 + o], None, ALU.mult)
                    nc.vector.tensor_scalar(w3[:, o, c], diag[:, :], cur[:, PARO + 7:PARO + 8], None, ALU.mult)
                    last = nc.vector.tensor_scalar(w3[:, 3, c], diag[:, :], cur[:, PARO + 7:PARO + 8], None, ALU.mult)
                last.then_inc(mats_ready, 1)
                dve.wait_ge(k1_ps, gi + 1)
                nc.vector.tensor_copy(cst[:, 0:1], ps[0:GP, PA, 0:1])
                nc.vector.tensor_scalar(cst[:, 1:3], ps[0:GP, PA, 1:3], cur[:, PARO + 12:PARO + 13], None, ALU.add).then_inc(k1_ready, 1)
                dve.wait_ge(k2_ps, gi + 1)
                nc.vector.tensor_scalar(cst[:, 3:5], ps[0:GP, PA + 1, 0:2], cur[:, PARO + 13:PARO + 14], None, ALU.add).then_inc(k2_ready, 1)
                dve.wait_ge(k3_ps, gi + 1)
                nc.vector.tensor_scalar(cst[:, 5:7], ps[0:GP, PA + 2, 0:2], cur[:, PARO + 14:PARO + 15], None, ALU.add).then_inc(k3_ready, 1)
                dve.wait_ge(k3_ready, gi + 1)

            def cols(ap, ch):
                return ap[:, 0:ch * HALF].rearrange("p (a n) -> p a n", n=HALF)

            def z1(gi, it, side, par, ch):
                u = gi * NU + 2 * it + side
                dve.wait_ge(a_done, u + 1)
                if not (isinstance(it, int) and it == 0):
                    dve.wait_ge(b_done, u - 1)
                nc.vector.scalar_tensor_tensor(out=cols(zb[:, side, :], ch), in0=cols(xr[:, par, :], ch), scalar=cst[:, 0:1],
                                               in1=ps[0:GP, PA:PA + ch, :], op0=ALU.mult, op1=ALU.add).then_inc(z1_done, 1)

            def h1(gi, it, side, ch):
                u = gi * NU + 2 * it + side
                dve.wait_ge(t1_done, u + 1)
                m = ch * HALF
                nc.vector.scalar_tensor_tensor(out=zb[:, side, 0:m], in0=t12[:, side, 0:m], scalar=cur[:, PARO + 9:PARO + 10],
                                               in1=zb[:, side, 0:m], op0=ALU.mult, op1=ALU.add).then_inc(h1_done, 1)

            def h2(gi, it, side, ch):
                u = gi * NU + 2 * it + side
                dve.wait_ge(t2_done, u + 1)
                if not (isinstance(it, int) and it == 0):
                    dve.wait_ge(c_done, u - 1)
                nc.vector.scalar_tensor_tensor(out=cols(hb[:, side, :], ch), in0=cols(t12[:, side, :], ch),
                                               scalar=cur[:, PARO + 10:PARO + 11], in1=ps[0:GP, PB:PB + ch, :],
                                               op0=ALU.mult, op1=ALU.add).then_inc(h2_done, 1)

            def fin_lo(gi, it):
                k = gi * NIT + it
                dve.wait_ge(c_done, gi * NU + 2 * it + 1)
                dve.wait_ge(sl_done, k)
                nc.vector.tensor_scalar(lo_c[:, :], ps[0:GP, PC, :], cst[:, 5:6], None, ALU.add).then_inc(lo_done, 1)

            def fin_sl(gi, it):
                k = gi * NIT + it
                dve.wait_ge(sgn_done, k + 1)
                dve.wait_ge(sig_done, k)
                nc.vector.tensor_tensor(sul[:, 0, :], lo_c[:, :], sgn[:, :], ALU.mult).then_inc(sl_done, 1)

            def fin_res(gi, it, par):
                if isinstance(it, int):
                    dve.wait_ge(xd_loaded[par], gi * (48 * (6 - par)) + 48 * (it // 2 + 1))
                    dve.wait_ge(res_stored[par], gi * (16 * (17 if par == 0 else 15)) + 48 * (it // 2))
                else:
                    dve.wait_ge(xd_loaded[par], gi * (48 * (6 - par)) + (it - par) * 24 + 48)
                    dve.wait_ge(res_stored[par], gi * (16 * (17 if par == 0 else 15)) + (it - par) * 24)
                dve.wait_ge(lik_done, gi * NIT + it + 1)
                nc.vector.scalar_tensor_tensor(out=res[:, par, :], in0=lik[:, :], scalar=BOUND, in1=xd[:, par, :],
                                               op0=ALU.max, op1=ALU.add).then_inc(res_all, 1)

            def body(gi, it, par):
                ch = chunks_of(it)
                if has(it - 2):
                    fin_lo(gi, it - 2)
                if has(it):
                    z1(gi, it, 0, par, ch)
                    h1(gi, it, 0, ch)
                if has(it - 2):
                    fin_sl(gi, it - 2)
                if has(it - 1):
                    h2(gi, it - 1, 1, chunks_of(it - 1))
                if has(it):
                    z1(gi, it, 1, par, ch)
                if has(it):
                    h1(gi, it, 1, ch)
                    h2(gi, it, 0, ch)
                if has(it - 2):
                    fin_res(gi, it - 2, par)

            with dve.Fori(0, NG) as gi:
                prepare(gi)
                body(gi, 0, 0)
                body(gi, 1, 1)
                with dve.Fori(1, 5) as p:
                    body(gi, 2 * p, 0)
                    body(gi, 2 * p + 1, 1)
                body(gi, 10, 0)
                body(gi, 11, 1)
                body(gi, 12, 0)


def has(it):
    return not isinstance(it, int) or 0 <= it < NIT


def chunks_of(it):
    return LASTC if isinstance(it, int) and it == NIT - 1 else 3


_W = "L0_conv_"
_E = "L1_conv_"


def lay_out(inputs):
    import numpy as np
    f = {k: np.asarray(v) for k, v in inputs.items()}
    a = {"x": np.ascontiguousarray(f["x"]).reshape(ROWS, NPX)}
    order = np.concatenate([np.arange(CH) + h * CH + part * C for h in range(HEADS) for part in range(2)] + [np.arange(2 * C, 3 * C)])
    wt = f[_W + "w_qkv"][order].T
    a["wqkv"] = np.concatenate([wt, wt[:, 512:576]], axis=1)
    wd = f[_W + "w_dw"].reshape(3 * C, 9)[order]
    a["wdw"] = np.stack([wd[0:128], wd[128:256], wd[256:384], wd[384:512], np.concatenate([wd[512:576], wd[512:576]])], axis=1)
    a["wproj"] = f[_W + "w_proj"].T.reshape(HEADS, CH, C).transpose(1, 0, 2)
    a["temp"] = np.tile(f[_W + "temperature"].reshape(1, HEADS), (CH, 1))
    grp = np.zeros((C, 256), np.float32)
    for c in range(C):
        g = c // 6 * 6
        grp[c, g:g + 6] = np.float32(1.0 / 6.0)
    a["grp"] = grp
    a["ident"] = np.eye(128, dtype=np.float32)
    a["diag"] = np.tile(np.eye(G, dtype=np.float32), (3, 1))
    cols = []
    for fl in range(3):
        m = [f[_E + "m0"][:, fl, 0]] + [f[_E + "m1"][:, o, fl] for o in range(3)] + [f[_E + "m2"][:, o, fl] for o in range(3)]
        m += [f[_E + "m3"][:, 0, fl]]
        m += [f[_E + f"f{i}"][:, fl, 0] for i in range(3)]
        m += [f[_E + f"b{i}"][:, fl, 0] for i in range(3)] + [f[_E + "b3"][:, 0, 0]]
        rows = np.tile(np.stack(m, axis=1), (NB, 1))
        rows = np.concatenate([rows, np.zeros((NG * G - ROWS, NPAR), np.float32)])
        cols.append(rows.reshape(NG, G, NPAR).transpose(1, 0, 2))
    a["par"] = np.concatenate(cols)
    return {k: np.ascontiguousarray(v) for k, v in a.items()}


_INS = ["x", "wqkv", "wdw", "wproj", "temp", "grp", "ident", "diag", "par"]


def kernel(**inputs):
    import concourse.bacc as _bacc
    from concourse import mybir as _mybir
    from concourse.bass_utils import run_bass_kernel_spmd as _run

    nc = _bacc.Bacc("TRN2", target_bir_lowering=False, num_devices=1)
    laid = lay_out(inputs)
    arrays, args = {}, []
    for name in _INS:
        a = laid[name]
        arrays[f"in_{name}_dram"] = a
        args.append(nc.dram_tensor(f"in_{name}_dram", a.shape, _mybir.dt.from_np(a.dtype), kind="ExternalInput").ap())
    args.append(nc.dram_tensor("out_0_dram", (ROWS, NPX), _mybir.dt.float32, kind="ExternalOutput").ap())
    build(nc, *args)
    r = _run(nc, [arrays], core_ids=[0])
    return r.results[0]["out_0_dram"].reshape(NB, C, H, W)
```

```python
import concourse.bass as bass
from concourse import mybir
from contextlib import ExitStack

F32 = mybir.dt.float32
ACT = mybir.ActivationFunctionType
ALU = mybir.AluOpType
AX = mybir.AxisListType

NB, C, H, W = 8, 192, 128, 128
NPX = H * W
CA, CB = 128, C - 128
HEADS = 4
CH = C // HEADS
RB = 8
BLK = RB * W
NBLK = H // RB
PW = W + 2
NT = 4
TAPS = [0, 1, 2, 3, 5, 6, 7, 8]
HALF = 512
GN_EPS = 1e-5
EPS = 1e-12

G = 42
GP = 3 * G
ROWS = NB * C
NG = -(-ROWS // G)
GLAST = ROWS - (NG - 1) * G
TW = 3 * HALF
NIT = -(-NPX // TW)
LASTC = (NPX - (NIT - 1) * TW) // HALF
NIN = 41
NC_ = 19
HB = NBLK // 2
BOUND = 1e-6


def at(start, n):
    return slice(start, start + n) if isinstance(start, int) else bass.ds(start, n)


def ge(eng, sem, n):
    if not isinstance(n, int) or n > 0:
        eng.wait_ge(sem, n)


def build(nc, x, wqkv, wdw, wproj, temp, grp, ident_in, diag_in, par, out):
    v_dram = nc.dram_tensor("v_scratch", (NB, C, NPX), F32, kind="Internal").ap()
    x1_dram = nc.dram_tensor("x1_scratch", (ROWS, NPX), F32, kind="Internal").ap()
    st_dram = nc.dram_tensor("stats_scratch", (NG * G, 2), F32, kind="Internal").ap()

    ctx = ExitStack()
    with ctx:
        def sem(name):
            return ctx.enter_context(nc.semaphore(name))

        ps = ctx.enter_context(nc.psum_tensor("ps", [128, 8, HALF], F32))
        zt = ctx.enter_context(nc.sbuf_tensor("zt", [128, 4 * PW], F32))
        ident = ctx.enter_context(nc.sbuf_tensor("ident", [128, 128], F32))
        diag = ctx.enter_context(nc.sbuf_tensor("diag", [GP, G], F32))

        l0 = ExitStack()

        def sb0(name, shape):
            return l0.enter_context(nc.sbuf_tensor(name, shape, F32))

        wq_a, wq_b = sb0("wq_a", [CA, 640]), sb0("wq_b", [CB, 640])
        ws_a, ws_b = sb0("ws_a", [CA, 640]), sb0("ws_b", [CB, 640])
        dwc = sb0("dwc", [128, 5, 9])
        band = sb0("band", [128, 6, 128])
        grp_a, grp_b = sb0("grp_a", [CA, 256]), sb0("grp_b", [2 * CB, 256])
        wp = sb0("wp", [CH, HEADS, C])
        tmp_bc = sb0("temp_bc", [CH, HEADS])
        xa, xb = sb0("xa", [CA, 2, BLK]), sb0("xb", [CB, 2, BLK])
        sxa, sxb = sb0("sxa", [CA, 2, BLK]), sb0("sxb", [2 * CB, 2, HALF])
        yxa, yxb = sb0("yxa", [CA, 2, BLK]), sb0("yxb", [2 * CB, 2, HALF])
        va, vb = sb0("va", [CA, 2, BLK]), sb0("vb", [CB, 2, BLK])
        xra, xrb = sb0("xra", [CA, W]), sb0("xrb", [CB, W])
        pbuf = sb0("pbuf", [128, 2, NT, RB + 2, PW])
        p4 = sb0("p4", [128, 2, RB // 2 + 1, PW])
        acc = sb0("acc", [128, 2, NT, BLK])
        acc4 = sb0("acc4", [128, 2, BLK // 2])
        qkt = sb0("qkt", [128, 2, 384])
        sx_bs = [sb0("sx_bs_a", [CA, 2 * NBLK, 6]), sb0("sx_bs_b", [2 * CB, NBLK, 6])]
        sy_bs = [sb0("sy_bs_a", [CA, 2 * NBLK, 6]), sb0("sy_bs_b", [2 * CB, NBLK, 6])]
        mv = sb0("mv", [128, 2, 2])
        gs = sb0("gs", [128, 8, 2])
        rout = sb0("rout", [128, 2, 2])
        bias = sb0("bias", [128, 5])
        gram = sb0("gram", [96, HEADS, 96])
        gtmp = sb0("gtmp", [96, HEADS, 96])
        nrm = sb0("nrm", [96, 8, HEADS])
        att = sb0("att", [CH, 3, HEADS, CH])
        apad = sb0("apad", [CH, HEADS, C])
        pt_a, pt_b = sb0("pt_a", [CA, C]), sb0("pt_b", [CB, C])
        l0.close()

        def sb1(name, shape):
            return ctx.enter_context(nc.sbuf_tensor(name, shape, F32))

        tab = sb1("tab", [GP, NG, NIN])
        sta = sb1("sta", [GP, NG, 2])
        sp_e, sp_u, sp_l, sp_m = (sb1(n, [GP, NG, 24]) for n in ("sp_e", "sp_u", "sp_l", "sp_m"))
        cc = sb1("cc", [GP, NG, NC_])
        t3 = sb1("t3", [GP, NG, 3])
        k0 = sb1("k0", [GP, NG, 3])
        k1 = sb1("k1", [GP, NG, 2, 3])
        k2 = sb1("k2", [GP, NG, 2, 3])
        a0 = sb1("a0", [GP, NG, 3])
        c0 = sb1("c0", [GP, NG, 2, 3])
        cur = sb1("cur", [GP, 2, NC_])
        w1 = sb1("w1", [GP, 2, GP])
        w2 = sb1("w2", [GP, 2, GP])
        w3 = sb1("w3", [GP, 2, 3, GP])
        xr = sb1("xr", [GP, 2, TW])
        xd = sb1("xd", [GP, 2, HALF])
        t0b = sb1("t0b", [GP, 2, TW])
        t12 = sb1("t12", [GP, 2, TW])
        zb = sb1("zb", [GP, 2, TW])
        hb = sb1("hb", [GP, 2, TW])
        lo_c, up_c = sb1("lo_c", [GP, HALF]), sb1("up_c", [GP, HALF])
        ssum, sgn = sb1("ssum", [GP, HALF]), sb1("sgn", [GP, HALF])
        sul = sb1("sul", [GP, 2, HALF])
        sig = sb1("sig", [GP, 2, HALF])
        dif = sb1("dif", [GP, HALF])
        lik = sb1("lik", [GP, HALF])
        res = sb1("res", [GP, 2, HALF])
        K_S0, K_O0, K_W1, K_A1, K_C1, K_C2, K_C3, K_F1, K_F2, K_M2, K_M3 = 0, 1, 3, 6, 7, 9, 11, 13, 14, 15, 18

        def c1set(s):
            return ps[:, 2 * s:2 * s + 2, :]
        T4O, TR, GR = 4, 5, 7

        def y_banks(s, alone):
            return (4 * s, 4 * s + 2) if alone else (2 * ((1 + s + 5) % 2), 2 * ((1 + s + 6) % 2))
        PA, PB, PC = 0, 3, 6

        w_loaded = sem("w_loaded")
        zeroed = sem("zeroed")
        band_ready = sem("band_ready")
        x_loaded = [sem("x_loaded0"), sem("x_loaded1")]
        sx_loaded = [sem("sx_loaded0"), sem("sx_loaded1")]
        yx_loaded = [sem("yx_loaded0"), sem("yx_loaded1")]
        v_loaded = [sem("v_loaded0"), sem("v_loaded1")]
        row_loaded = sem("row_loaded")
        st_done = sem("st_done")
        c1_ready, evac_done = sem("c1_ready"), sem("evac_done")
        tap_done = sem("tap_done")
        dw_chain = sem("dw_chain")
        t4_done, t4_evac = sem("t4_done"), sem("t4_evac")
        tr_done, tr_evac, gr_done = sem("tr_done"), sem("tr_evac"), sem("gr_done")
        v_stored = [sem("v_stored0"), sem("v_stored1")]
        v4_stored = [sem("v4_stored0"), sem("v4_stored1")]
        ya_ready, yb_ready = sem("ya_ready"), sem("yb_ready")
        ya_done, yb_done = sem("ya_done"), sem("yb_done")
        y_stats = sem("y_stats")
        x1_stored = [sem("x1_stored0"), sem("x1_stored1")]
        gsteps = ["mv_marked", "mv_ready", "mg_ready", "dev_ready", "dsq_ready", "q_ready", "vg_ready", "ve_ready",
                  "sd_ready", "rstd_ready"]
        gx = {k: sem("gx_" + k) for k in gsteps}
        gy = {k: sem("gy_" + k) for k in gsteps}
        ws_ready, bias_ps, bias_ready = sem("ws_ready"), sem("bias_ps"), sem("bias_ready")
        stat_stored = sem("stat_stored")
        A = {k: sem("at_" + k) for k in [
            "gram", "diag", "n2", "n", "ne", "r1", "m", "m2", "r2", "s", "rows", "tps", "nq", "mx", "sub", "exp",
            "sum", "rs", "pad", "ptps", "pt"]}
        stats_loaded, tab_loaded, zrow_stored = sem("stats_loaded"), sem("tab_loaded"), sem("zrow_stored")
        tab_act, lin_chain = sem("tab_act"), sem("lin_chain")
        w3_zeroed = sem("w3_zeroed")
        cur_ready, mats_ready = sem("cur_ready"), sem("mats_ready")
        xr_loaded = [sem("xr_loaded0"), sem("xr_loaded1")]
        xd_loaded = [sem("xd_loaded0"), sem("xd_loaded1")]
        t0_done, a_done, z1_done, t1_done, h1_done = (sem(n) for n in ("t0_done", "a_done", "z1_done", "t1_done", "h1_done"))
        b_done, t2_done, h2_done, c_done = (sem(n) for n in ("b_done", "t2_done", "h2_done", "c_done"))
        up_done, lo_done, sum_done, sgn_done, su_done, sl_done, sig_done, dif_done = (sem(n) for n in (
            "up_done", "lo_done", "sum_done", "sgn_done", "su_done", "sl_done", "sig_done", "dif_done"))
        lik_done, res_all = sem("lik_done"), sem("res_all")
        res_stored = [sem("res_stored0"), sem("res_stored1")]

        block = ctx.enter_context(nc.Block())

        def images(eng, image):
            image(0, False, True)
            with eng.Fori(1, NB - 1) as b:
                image(b, True, True)
            image(NB - 1, True, False)

        def groups(eng, group):
            group(0, 0)
            with eng.Fori(0, (NG - 3) // 2) as q:
                group(2 * q + 1, 1)
                group(2 * q + 2, 0)
            group(NG - 2, 1)
            group(NG - 1, 0)

        def place(gi, gp, it):
            if not isinstance(it, int):
                return gp, 3
            if it < 0:
                return None if isinstance(gi, int) and gi == 0 else (1 - gp, LASTC if it == -1 else 3)
            if it >= NIT:
                return None if isinstance(gi, int) and gi == NG - 1 else (1 - gp, 3)
            return gp, LASTC if it == NIT - 1 else 3

        @block.sync
        def _(sp):
            for dst, src in ((wq_a[:, :], wqkv[0:CA, :]), (wq_b[:, :], wqkv[CA:C, :]), (dwc[:, :, :], wdw[:, :, :]),
                             (grp_a[:, :], grp[0:CA, :]), (grp_b[:, :], grp[CA:CA + 2 * CB, :]), (wp[:, :, :], wproj[:, :, :]),
                             (tmp_bc[:, :], temp[:, :]), (ident[:, :], ident_in[:, :]), (diag[:, :], diag_in[:, :])):
                sp.dma_start(dst, src).then_inc(w_loaded, 16)

            def col_of(j, s, off=0):
                return (2 * j + s) * BLK + off if isinstance(j, int) else sp.snap(j * (2 * BLK) + (s * BLK + off))

            def row_of(b, off=0):
                return b * C + off if isinstance(b, int) else sp.snap(b * C + off)

            def stats_load(b, ra, rb, j, s):
                cs = [col_of(j, s), col_of(j, s, HALF)]
                c = at(cs[0], BLK)
                ge(sp, st_done, b * NBLK + j * 2 + (s - 1))
                sp.dma_start(sxa[:, s, :], x[at(ra, CA), c]).then_inc(sx_loaded[s], 16)
                for h in range(2):
                    sp.dma_start(sxb[h * CB:h * CB + CB, s, :], x[at(rb, CB), at(cs[h], HALF)]).then_inc(sx_loaded[s], 16)

            def conv_load(b, ra, rb, j, s, rows):
                n = rows * W
                c = at(col_of(j, s, W), n)
                ge(sp, c1_ready, b * 81 + j * 10 + (5 * s - 4))
                sp.dma_start(xa[:, s, 0:n], x[at(ra, CA), c]).then_inc(x_loaded[s], 16)
                sp.dma_start(xb[:, s, 0:n], x[at(rb, CB), c]).then_inc(x_loaded[s], 16)

            def conv_store(b, j, s):
                c = at(col_of(j, s), BLK)
                bb = at(b, 1)
                sp.wait_ge(dw_chain, (b * NBLK + j * 2 + (s + 1)) * (NT * 8))
                sp.wait_ge(t4_evac, b * NBLK + j * 2 + (s + 1))
                for h in range(2):
                    dst = v_dram[bb, CA:C, c].rearrange("a p (r t w) -> (a p) r t w", t=2, w=W)[:, :, h, :]
                    sp.dma_start(dst, acc4[64 * h:64 * h + 64, s, :].rearrange("p (r w) -> p r w", w=W)
                                 ).then_inc(v4_stored[s], 16)
                sp.dma_start(v_dram[bb, 0:CA, c].rearrange("a p n -> (a p) n"), acc[:, s, 3, :]).then_inc(v_stored[s], 16)

            def proj_load(b, ra, rb, j, s, alone=False):
                cs = [col_of(j, s), col_of(j, s, HALF)]
                c = at(cs[0], BLK)
                bb = at(b, 1)
                if alone and not isinstance(j, int):
                    sp.wait_ge(yb_done, b * NBLK + j * 2 + (s - 1))
                elif not (isinstance(j, int) and j == 0):
                    sp.wait_ge(y_stats, b * NBLK + j * 2 + (s - 1))
                    sp.wait_ge(x1_stored[s], (b * HB + j) * 48)
                sp.dma_start(yxa[:, s, :], x[at(ra, CA), c]).then_inc(yx_loaded[s], 16)
                for h in range(2):
                    sp.dma_start(yxb[h * CB:h * CB + CB, s, :], x[at(rb, CB), at(cs[h], HALF)]).then_inc(yx_loaded[s], 16)
                sp.dma_start(va[:, s, :], v_dram[bb, 0:CA, c].rearrange("a p n -> (a p) n")).then_inc(v_loaded[s], 16)
                sp.dma_start(vb[:, s, :], v_dram[bb, CA:C, c].rearrange("a p n -> (a p) n")).then_inc(v_loaded[s], 16)

            def x1_store(b, ra, rb, j, s, oa=yxa, ob=yxb):
                cs = [col_of(j, s), col_of(j, s, HALF)]
                c = at(cs[0], BLK)
                sp.wait_ge(ya_done, b * NBLK + j * 2 + (s + 1))
                sp.dma_start(x1_dram[at(ra, CA), c], oa[:, s, :]).then_inc(x1_stored[s], 16)
                sp.wait_ge(yb_done, b * NBLK + j * 2 + (s + 1))
                for h in range(2):
                    sp.dma_start(x1_dram[at(rb, CB), at(cs[h], HALF)], ob[h * CB:h * CB + CB, s, :]).then_inc(x1_stored[s], 16)

            stats_load(0, 0, CA, 0, 0)
            stats_load(0, 0, CA, 0, 1)
            with sp.Fori(1, HB) as j:
                stats_load(0, 0, CA, j, 0)
                stats_load(0, 0, CA, j, 1)

            def first_loads(b, ra, rb):
                sp.dma_start(xra[:, :], x[at(ra, CA), 0:W]).then_inc(row_loaded, 16)
                sp.dma_start(xrb[:, :], x[at(rb, CB), 0:W]).then_inc(row_loaded, 16)
                for s in range(2):
                    conv_load(b, ra, rb, 0, s, RB)

            def v_complete(b):
                for s in range(2):
                    sp.wait_ge(v_stored[s], b * (16 * HB) + 16 * HB)
                    sp.wait_ge(v4_stored[s], b * (32 * HB) + 32 * HB)

            def x1_complete(b):
                taken, stored = b * NBLK + NBLK, b * (48 * HB) + 48 * HB
                if not isinstance(b, int):
                    taken, stored = sp.snap(taken), sp.snap(stored)
                for s in range(2):
                    sp.wait_ge(x1_stored[s], stored)
                sp.wait_ge(y_stats, taken)

            def image(b, has_y, has_next):
                ra, rb = row_of(b), row_of(b, CA)
                na, nb = row_of(b, C), row_of(b, C + CA)
                pa, pb = row_of(b, -C), row_of(b, CA - C)

                def turn(j, s, jp, sp_, last=False):
                    if not (isinstance(j, int) and j == 0):
                        conv_load(b, ra, rb, j, s, RB - 1 if last else RB)
                    if has_next:
                        stats_load(b + 1, na, nb, j, s)
                    if has_y:
                        if jp is None:
                            v_complete(b - 1)
                        proj_load(b - 1, pa, pb, j, s)
                    if jp is not None:
                        conv_store(b, jp, sp_)
                        if has_y:
                            x1_store(b - 1, pa, pb, jp, sp_)

                turn(0, 0, None, None)
                turn(0, 1, 0, 0)
                with sp.Fori(1, HB - 1) as j:
                    turn(j, 0, j - 1, 1)
                    turn(j, 1, j, 0)
                turn(HB - 1, 0, HB - 2, 1)
                turn(HB - 1, 1, HB - 1, 0, True)
                if has_y:
                    x1_store(b - 1, pa, pb, HB - 1, 1)
                    x1_complete(b - 1)
                if has_next:
                    first_loads(b + 1, na, nb)
                conv_store(b, HB - 1, 1)

            first_loads(0, 0, CA)
            images(sp, image)
            v_complete(NB - 1)
            ra, rb = (NB - 1) * C, (NB - 1) * C + CA
            proj_load(NB - 1, ra, rb, 0, 0, True)
            proj_load(NB - 1, ra, rb, 0, 1, True)
            with sp.Fori(1, HB) as j:
                for s in range(2):
                    proj_load(NB - 1, ra, rb, j, s, True)
                    x1_store(NB - 1, ra, rb, j - 1, s, sxa, sxb)
            for s in range(2):
                x1_store(NB - 1, ra, rb, HB - 1, s, sxa, sxb)

            x1_complete(NB - 1)
            sp.wait_ge(stat_stored, 32 * NB)
            sp.wait_ge(zrow_stored, 16)
            sp.wait_ge(gy["rstd_ready"], NB)
            sp.dma_start(tab[:, :, :], par[:, :, :]).then_inc(tab_loaded, 16)
            for f in range(3):
                sp.dma_start(sta[f * G:f * G + G, :, :], st_dram.rearrange("(i g) s -> g i s", g=G)).then_inc(stats_loaded, 16)

            def load_xr(gi, row, rows, n, it, s, chunks=3):
                col = it * TW if isinstance(it, int) else sp.snap(it * TW)
                ge(sp, z1_done, n * 2 - 2)
                for f in range(3):
                    sp.dma_start(xr[f * G:f * G + rows, s, 0:chunks * HALF], x1_dram[at(row, rows), at(col, chunks * HALF)]
                                 ).then_inc(xr_loaded[s], 16)

            def load_xd(row, rows, it, s, chunks=3):
                cs = [it * TW + c * HALF if isinstance(it, int) else sp.snap(it * TW + c * HALF) for c in range(chunks)]
                for c in range(3):
                    sp.dma_start(xd[c * G:c * G + rows, s, :], x1_dram[at(row, rows), at(cs[min(c, chunks - 1)], HALF)]
                                 ).then_inc(xd_loaded[s], 16)

            def store(row, rows, n, it, s, chunks=3):
                pieces = [(c, c * HALF, 0, HALF) for c in range(chunks)]
                if chunks < 3:
                    c, o, _, _ = pieces.pop()
                    pieces += [(c, o, 0, HALF // 2), (c, o + HALF // 2, HALF // 2, HALF // 2)]
                cs = [it * TW + o if isinstance(it, int) else sp.snap(it * TW + o) for _, o, _, _ in pieces]
                sp.wait_ge(res_all, n + 1)
                for (c, _, o, m), col in zip(pieces, cs):
                    sp.dma_start(out[at(row, rows), at(col, m)], res[c * G:c * G + rows, s, o:o + m]).then_inc(res_stored[s], 16)

            def group(gi, gp):
                static = isinstance(gi, int)
                row = gi * G if static else sp.snap(gi * G)
                rowp = (gi - 1) * G if static else sp.snap(gi * G - G)
                rown = (gi + 1) * G if static else sp.snap(gi * G + G)
                rows = GLAST if static and gi == NG - 1 else G
                nrows = GLAST if static and gi == NG - 2 else G
                n0 = gi * NIT

                def turn(it, s):
                    n = n0 + it
                    if isinstance(it, int) and it + 2 >= NIT:
                        if not (static and gi == NG - 1):
                            load_xr(gi, rown, nrows, n + 2, it + 2 - NIT, s)
                    else:
                        load_xr(gi, row, rows, n + 2, it + 2, s, LASTC if isinstance(it, int) and it + 2 == NIT - 1 else 3)
                    if isinstance(it, int) and it < 2:
                        if not (static and gi == 0):
                            store(rowp, G, n - 2, NIT + it - 2, s, LASTC if it == 1 else 3)
                    else:
                        store(row, rows, n - 2, it - 2, s)
                    load_xd(row, rows, it, s, LASTC if isinstance(it, int) and it == NIT - 1 else 3)

                if static and gi == 0:
                    load_xr(0, row, rows, 0, 0, 0)
                    load_xr(0, row, rows, 1, 1, 1)
                turn(0, gp)
                turn(1, 1 - gp)
                with sp.Fori(1, 4) as p:
                    turn(2 * p, gp)
                    turn(2 * p + 1, 1 - gp)
                turn(8, gp)
                turn(9, 1 - gp)
                turn(10, gp)
                if static and gi == NG - 1:
                    store(row, rows, n0 + NIT - 2, NIT - 2, 1 - gp)
                    store(row, rows, n0 + NIT - 1, NIT - 1, gp, LASTC)

            groups(sp, group)
            sp.wait_ge(res_stored[0], 48 * ((NG * NIT + 1) // 2))
            sp.wait_ge(res_stored[1], 48 * (NG * NIT // 2))
            sp.drain()

        @block.gpsimd
        def _(pool):
            nc.gpsimd.memset(zt[:, :], 0.0).then_inc(zeroed, 1)
            nc.gpsimd.memset(pbuf[:, :, :, :, :], 0.0)
            nc.gpsimd.memset(p4[:, :, :, :], 0.0)
            nc.gpsimd.memset(mv[:, :, :], 0.0)
            nc.gpsimd.memset(apad[:, :, :], 0.0)
            nc.gpsimd.memset(band[:, :, :], 0.0).then_inc(zeroed, 1)
            pool.wait_ge(zeroed, 1)
            pool.dma_start(st_dram[ROWS:NG * G, :], zt[0:NG * G - ROWS, 0:2]).then_inc(zrow_stored, 16)

            def fin(n):
                pool.wait_ge(up_done, n + 1)
                pool.wait_ge(lo_done, n + 1)
                ge(pool, sgn_done, n)
                nc.gpsimd.tensor_tensor(ssum[:, :], lo_c[:, :], up_c[:, :], ALU.add).then_inc(sum_done, 1)
                pool.wait_ge(sgn_done, n + 1)
                ge(pool, sig_done, n)
                nc.gpsimd.tensor_tensor(sul[:, 1, :], up_c[:, :], sgn[:, :], ALU.mult).then_inc(su_done, 1)
                pool.wait_ge(sig_done, n + 1)
                ge(pool, lik_done, n)
                nc.gpsimd.tensor_tensor(dif[:, :], sig[:, 1, :], sig[:, 0, :], ALU.subtract).then_inc(dif_done, 1)

            fin(0)
            with pool.Fori(1, NG * NIT) as n:
                fin(n)

        @block.scalar
        def _(act):
            act.wait_ge(zeroed, 2)

            def group_sqrt(g, b):
                act.wait_ge(g["ve_ready"], b + 1)
                nc.scalar.activation(gs[:, 4, :], gs[:, 3, :], ACT.Sqrt).then_inc(g["sd_ready"], 1)

            def stats_out(b):
                ra, rb = (b * C, b * C + CA) if isinstance(b, int) else (act.snap(b * C), act.snap(b * C + CA))
                act.wait_ge(gy["rstd_ready"], b + 1)
                for t, r0, rn in ((0, ra, CA), (1, rb, CB)):
                    act.dma_start(st_dram[at(r0, rn), :], rout[0:rn, t, :]).then_inc(stat_stored, 16)

            group_sqrt(gx, 0)

            def image(b, has_y, has_next):
                b1 = b + 1
                act.wait_ge(bias_ps, b1)
                if has_y:
                    act.wait_ge(c1_ready, b * 81)
                nc.scalar.activation(bias[:, :], ps[:, T4O, 4:9], ACT.Identity).then_inc(bias_ready, 1)
                act.wait_ge(bias_ready, b1)
                ge(act, dw_chain, b * (NBLK * NT * 8))
                ge(act, t4_done, b * NBLK)
                nc.scalar.activation(pbuf[:, 0, :, 0, :], zt[:, :].rearrange("p (t w) -> p t w", w=PW), ACT.Copy)
                nc.scalar.activation(p4[0:64, 0, 0, :], zt[0:64, 0:PW], ACT.Copy)
                act.wait_ge(c1_ready, b * 81 + 1)
                for t in range(NT):
                    nc.scalar.activation(pbuf[:, 0, t, 1, 1:1 + W], ps[:, 0, t * W:t * W + W], ACT.Identity, bias=bias[:, t:t + 1])
                nc.scalar.activation(p4[64:128, 0, 0, 1:1 + W], ps[64:128, 1, 0:W], ACT.Identity,
                                     bias=bias[64:128, 4:5]).then_inc(evac_done, 1)
                if has_y:
                    act.wait_ge(A["sub"], b)
                    nc.scalar.activation(att[:, 2, :, :], att[:, 1, :, :], ACT.Exp).then_inc(A["exp"], 1)

                def step(j, s, first, last):
                    n16 = b * NBLK + j * 2 + s
                    seq = b * 81 + j * 10 + (5 * s + 1)
                    if not (isinstance(j, int) and j == 0):
                        act.wait_ge(dw_chain, (n16 - 1) * (NT * 8))
                        act.wait_ge(t4_done, n16 - 1)
                    if not first:
                        act.wait_ge(evac_done, seq)
                        nc.scalar.activation(pbuf[:, s, :, 0:2, :], pbuf[:, 1 - s, :, RB:RB + 2, :], ACT.Copy)
                        nc.scalar.activation(p4[:, s, 0, :], p4[:, 1 - s, RB // 2, :], ACT.Copy)
                    if last:
                        nc.scalar.activation(pbuf[:, s, :, RB + 1, :], zt[:, :].rearrange("p (t w) -> p t w", w=PW), ACT.Copy)
                        nc.scalar.activation(p4[64:128, s, RB // 2, :], zt[64:128, 0:PW], ACT.Copy)
                    rows = RB - 1 if last else RB
                    for k in range(5):
                        cs = (1 + s + k) % 2
                        src = c1set(cs).rearrange("p a (r w) -> p (a r) w", w=W)
                        act.wait_ge(c1_ready, seq + k + 1)
                        if k == 0:
                            nh = RB // 2 - 1 if last else RB // 2
                            nc.scalar.activation(p4[0:64, s, 1:, 1:1 + W], src[0:64, 0:RB:2, :], ACT.Identity, bias=bias[0:64, 4:5])
                            nc.scalar.activation(p4[64:128, s, 1:1 + nh, 1:1 + W], src[64:128, 1:2 * nh:2, :], ACT.Identity,
                                                 bias=bias[64:128, 4:5]).then_inc(evac_done, 1)
                        else:
                            t = k - 1
                            nc.scalar.activation(pbuf[:, s, t, 2:2 + rows, 1:1 + W], src[:, 0:rows, :], ACT.Identity,
                                                 bias=bias[:, t:t + 1]).then_inc(evac_done, 1)
                            if t == 0 and not (isinstance(j, int) and j == 0):
                                act.wait_ge(tr_done, (n16 - 1) * 8)
                            if t == 3:
                                ge(act, v_stored[s], (b * HB + j) * 16)
                            act.wait_ge(evac_done, seq + k + 1)
                            nc.scalar.activation(acc[:, s, t, :].rearrange("p (r w) -> p r w", w=W),
                                                 pbuf[:, s, t, 1:1 + RB, 1:1 + W], ACT.Copy, scale=dwc[:, t, 4:5]).then_inc(tap_done, 1)
                    act.wait_ge(t4_done, n16 + 1)
                    ge(act, v4_stored[s], (b * HB + j) * 32)
                    nc.scalar.activation(acc4[:, s, :], ps[:, T4O, :], ACT.Copy).then_inc(t4_evac, 1)

                def evac_transposed(j, s, first):
                    base = b * 128 + j * 16 + 8 * s
                    for c in range(8):
                        act.wait_ge(tr_done, base + c + 1)
                        if not (first and c < 2):
                            act.wait_ge(gr_done, base + c - 1)
                        nc.scalar.activation(qkt[:, c % 2, :], ps[:, TR + c % 2, 0:384], ACT.Copy).then_inc(tr_evac, 1)

                def y_evac(j, s):
                    if has_y:
                        ya, _ = y_banks(s, False)
                        act.wait_ge(ya_ready, (b - 1) * NBLK + j * 2 + (s + 1))
                        nc.scalar.activation(yxa[:, s, :].rearrange("p (a n) -> p a n", a=2), ps[:, ya:ya + 2, :],
                                             ACT.Copy).then_inc(ya_done, 1)

                step(0, 0, True, False)
                y_evac(0, 0)
                step(0, 1, False, False)
                evac_transposed(0, 0, True)
                y_evac(0, 1)
                with act.Fori(1, HB - 1) as j:
                    step(j, 0, False, False)
                    evac_transposed(j - 1, 1, False)
                    y_evac(j, 0)
                    step(j, 1, False, False)
                    evac_transposed(j, 0, False)
                    y_evac(j, 1)
                J = HB - 1
                step(J, 0, False, False)
                evac_transposed(J - 1, 1, False)
                y_evac(J, 0)
                step(J, 1, False, True)
                evac_transposed(J, 0, False)
                y_evac(J, 1)
                if has_y:
                    group_sqrt(gy, b - 1)
                    stats_out(b - 1)
                if has_next:
                    group_sqrt(gx, b + 1)
                evac_transposed(J, 1, False)
                act.wait_ge(A["n2"], b1)
                nc.scalar.activation(nrm[:, 1, :], nrm[:, 0, :], ACT.Sqrt).then_inc(A["n"], 1)

            images(act, image)
            act.wait_ge(A["sub"], NB)
            nc.scalar.activation(att[:, 2, :, :], att[:, 1, :, :], ACT.Exp).then_inc(A["exp"], 1)
            group_sqrt(gy, NB - 1)
            stats_out(NB - 1)

            act.wait_ge(tab_loaded, 16)
            nc.scalar.activation(tab[:, :, 24:27], tab[:, :, 24:27], ACT.Tanh)
            nc.scalar.activation(sp_e[:, :, :], tab[:, :, 0:24], ACT.Abs).then_inc(tab_act, 1)
            act.wait_ge(tab_act, 1)
            nc.scalar.activation(sp_e[:, :, :], sp_e[:, :, :], ACT.Exp, scale=-1.0).then_inc(tab_act, 1)
            act.wait_ge(lin_chain, 1)
            nc.scalar.activation(sp_l[:, :, :], sp_u[:, :, :], ACT.Ln).then_inc(tab_act, 1)
            nc.scalar.preload_act_table(ACT.Sigmoid)

            def t0(n, side, par, w):
                gp, ch = w
                if side == 0:
                    act.wait_ge(xr_loaded[par], (n - par) * 24 + 48)
                ge(act, a_done, n * 2 + side - 1)
                m = ch * HALF
                nc.scalar.activation(t0b[:, side, 0:m], xr[:, par, 0:m], ACT.Tanh, scale=cur[:, gp, K_S0:K_S0 + 1],
                                     bias=cur[:, gp, K_O0 + side:K_O0 + side + 1]).then_inc(t0_done, 1)

            def t1(n, side, w):
                gp, ch = w
                u = n * 2 + side
                act.wait_ge(z1_done, u + 1)
                ge(act, h2_done, u - 1)
                m = ch * HALF
                nc.scalar.activation(t12[:, side, 0:m], zb[:, side, 0:m], ACT.Tanh,
                                     bias=cur[:, gp, K_C1 + side:K_C1 + side + 1]).then_inc(t1_done, 1)

            def t2(n, side, w):
                gp, ch = w
                act.wait_ge(b_done, n * 2 + side + 1)
                nc.scalar.activation(t12[:, side, 0:ch * HALF].rearrange("p (a n) -> p a n", n=HALF), ps[0:GP, PB:PB + ch, :],
                                     ACT.Tanh, bias=cur[:, gp, K_C2 + side:K_C2 + side + 1]).then_inc(t2_done, 1)

            def fin_up(n, w):
                act.wait_ge(c_done, n * 2 + 2)
                ge(act, su_done, n)
                nc.scalar.activation(up_c[:, :], ps[0:GP, PC + 1, :], ACT.Identity,
                                     bias=cur[:, w[0], K_C3 + 1:K_C3 + 2]).then_inc(up_done, 1)

            def fin_sign(n):
                act.wait_ge(sum_done, n + 1)
                ge(act, sl_done, n)
                ge(act, su_done, n)
                nc.scalar.activation(sgn[:, :], ssum[:, :], ACT.Sign).then_inc(sgn_done, 1)

            def fin_sigmoid(n):
                act.wait_ge(su_done, n + 1)
                act.wait_ge(sl_done, n + 1)
                ge(act, dif_done, n)
                nc.scalar.activation(sig[:, :, :], sul[:, :, :], ACT.Sigmoid, scale=-1.0).then_inc(sig_done, 1)

            def fin_abs(n):
                act.wait_ge(dif_done, n + 1)
                ge(act, res_all, n)
                nc.scalar.activation(lik[:, :], dif[:, :], ACT.Abs).then_inc(lik_done, 1)

            def body(gi, gp, it, par):
                n = gi * NIT + it
                w, w1_, w2_, wn = (place(gi, gp, i) for i in (it, it - 1, it - 2, it + 1))
                t0(n, 1, par, w)
                if w2_:
                    fin_up(n - 2, w2_)
                t1(n, 0, w)
                if w1_:
                    t2(n - 1, 1, w1_)
                if w2_:
                    fin_sign(n - 2)
                if wn:
                    if isinstance(it, int) and it == NIT - 1:
                        act.wait_ge(mats_ready, gi + 2)
                    t0(n + 1, 0, 1 - par, wn)
                if w2_:
                    fin_sigmoid(n - 2)
                t1(n, 1, w)
                if w2_:
                    fin_abs(n - 2)
                t2(n, 0, w)

            def group(gi, gp):
                if isinstance(gi, int) and gi == 0:
                    act.wait_ge(mats_ready, 1)
                    t0(0, 0, 0, (0, 3))
                body(gi, gp, 0, gp)
                body(gi, gp, 1, 1 - gp)
                first = 1
                if isinstance(gi, int) and gi == 0:
                    body(0, 0, 2, 0)
                    body(0, 0, 3, 1)
                    first = 2
                with act.Fori(first, 5) as p:
                    body(gi, gp, 2 * p, gp)
                    body(gi, gp, 2 * p + 1, 1 - gp)
                body(gi, gp, 10, gp)
                if isinstance(gi, int) and gi == NG - 1:
                    tail(gi, gp)

            def tail(gi, gp):
                n = gi * NIT + NIT
                fin_up(n - 2, (gp, 3))
                t2(n - 1, 1, (gp, LASTC))
                fin_sign(n - 2)
                fin_sigmoid(n - 2)
                fin_abs(n - 2)
                fin_up(n - 1, (gp, LASTC))
                fin_sign(n - 1)
                fin_sigmoid(n - 1)
                fin_abs(n - 1)

            groups(act, group)

        @block.tensor
        def _(pe):
            pe.wait_ge(w_loaded, 16 * 9)
            pe.wait_ge(band_ready, 1)

            def mm(o, l, r, start=True, stop=True, **kw):
                return nc.tensor.matmul(o, l, r, start=start, stop=stop, **kw)

            def group_means(g, src, col, ready, done, b):
                pe.wait_ge(g[ready], b + 1)
                for t in range(2):
                    mm(ps[:, T4O, col + t:col + t + 1], grp_a[:, t * 128:t * 128 + 128], src[:, 0:1], stop=False)
                    last = mm(ps[:, T4O, col + t:col + t + 1], grp_b[:, t * 128:t * 128 + 128], src[:, 1:2], start=False)
                last.then_inc(g[done], 1)

            def group_norm(g, b):
                group_means(g, mv[:, :, 0], 0, "mv_ready", "mg_ready", b)
                group_means(g, gs[:, 2, :], 2, "q_ready", "vg_ready", b)

            def proj(b, j, s, seq=None):
                n16 = b * NBLK + j * 2 + s
                ya, yb = y_banks(s, seq is None)
                pe.wait_ge(v_loaded[s], (b * HB + j) * 32 + 32)
                pe.wait_ge(A["pt"], b + 1)
                if seq is not None:
                    pe.wait_ge(evac_done, seq + 4)
                elif not (isinstance(j, int) and j == 0):
                    pe.wait_ge(yb_done, n16 - 1)
                for h in range(2):
                    mm(ps[:, ya + h, :], pt_a[:, 0:CA], va[:, s, h * HALF:h * HALF + HALF], stop=False)
                    last = mm(ps[:, ya + h, :], pt_b[:, 0:CA], vb[:, s, h * HALF:h * HALF + HALF], start=False, stop=seq is None)
                if seq is not None:
                    pe.wait_ge(yx_loaded[s], (b * HB + j) * 48 + 48)
                    for h in range(2):
                        last = mm(ps[:, ya + h, :], ident[:, :], yxa[:, s, h * HALF:h * HALF + HALF], start=False)
                last.then_inc(ya_ready, 1)
                if seq is not None:
                    pe.wait_ge(evac_done, seq + 5)
                for h in range(2):
                    o = ps[CB * h:CB * h + CB, yb, :]
                    mm(o, pt_a[:, CA:C], va[:, s, h * HALF:h * HALF + HALF], stop=False)
                    last = mm(o, pt_b[:, CA:C], vb[:, s, h * HALF:h * HALF + HALF], start=False)
                last.then_inc(yb_ready, 1)

            def attn_transpose(b):
                pe.wait_ge(A["rows"], b + 1)
                for h in range(HEADS):
                    last = nc.tensor.transpose(ps[0:96, TR, h * 96:h * 96 + 96], gtmp[:, h, :], ident[0:96, 0:96])
                last.then_inc(A["tps"], 1)

            def attn_proj(b):
                pe.wait_ge(A["pad"], b + 1)
                for h in range(HEADS):
                    mm(ps[:, TR + 1, 0:C], apad[:, h, 0:CA], wp[:, h, :], start=h == 0, stop=h == HEADS - 1)
                for h in range(HEADS):
                    last = mm(ps[0:CB, TR, 0:C], apad[:, h, CA:C], wp[:, h, :], start=h == 0, stop=h == HEADS - 1)
                last.then_inc(A["ptps"], 1)

            group_norm(gx, 0)

            def image(b, has_y, has_next):
                b1 = b + 1
                pe.wait_ge(ws_ready, b1)
                for t in range(5):
                    mm(ps[:, T4O, 4 + t:5 + t], ws_a[:, t * 128:t * 128 + 128], gs[:, 5, 0:1], stop=False)
                    last = mm(ps[:, T4O, 4 + t:5 + t], ws_b[:, t * 128:t * 128 + 128], gs[0:CB, 5, 1:2], start=False)
                last.then_inc(bias_ps, 1)
                pe.wait_ge(row_loaded, b * 32 + 32)
                for t in range(5):
                    o = ps[:, 0, t * W:t * W + W] if t < NT else ps[:, 1, 0:W]
                    mm(o, ws_a[:, t * 128:t * 128 + 128], xra[:, :], stop=False)
                    last = mm(o, ws_b[:, t * 128:t * 128 + 128], xrb[:, :], start=False)
                last.then_inc(c1_ready, 1)
                if has_y:
                    attn_transpose(b - 1)
                mm(ps[0:96, GR, 0:384], zt[:, 0:96], zt[:, 0:384])

                def conv1x1(j, s):
                    n16 = b * NBLK + j * 2 + s
                    seq = b * 81 + j * 10 + (5 * s + 1)
                    pe.wait_ge(x_loaded[s], (b * HB + j) * 32 + 32)
                    for k in range(5):
                        t = 4 if k == 0 else k - 1
                        cs = (1 + s + k) % 2
                        ge(pe, evac_done, seq + k - 1)
                        if has_y and k < 2 and not (isinstance(j, int) and j == 0 and s == 0):
                            ge(pe, ya_done if k == 0 else yb_done, n16 - NBLK)
                        for h in range(2):
                            o = ps[:, 2 * cs + h, :]
                            mm(o, ws_a[:, t * 128:t * 128 + 128], xa[:, s, h * HALF:h * HALF + HALF], stop=False)
                            last = mm(o, ws_b[:, t * 128:t * 128 + 128], xb[:, s, h * HALF:h * HALF + HALF], start=False)
                        last.then_inc(c1_ready, 1)

                def conv_tile4(j, s):
                    n16 = b * NBLK + j * 2 + s
                    seq = b * 81 + j * 10 + (5 * s + 1)
                    pe.wait_ge(evac_done, seq + 1)
                    ge(pe, t4_evac, n16)
                    pe.wait_ge(bias_ready, b1)
                    for k in range(6):
                        dx, blk = k % 3, k // 3
                        last = mm(ps[:, T4O, :], band[:, k, :], p4[:, s, blk:blk + RB // 2, dx:dx + W], start=k == 0, stop=k == 5)
                    last.then_inc(t4_done, 1)

                def transposes(j, s, c, first, last):
                    n16 = b * NBLK + j * 2 + s
                    base = b * 128 + j * 16 + 8 * s
                    if c == 0:
                        pe.wait_ge(dw_chain, (n16 + 1) * (NT * 8) - (8 if last else 1))
                    if first and has_y:
                        pe.wait_ge(A["pt"], b)
                    if not (first and c < 2):
                        pe.wait_ge(tr_evac, base + c - 1)
                    for t in range(3):
                        last = nc.tensor.transpose(ps[:, TR + c % 2, t * 128:t * 128 + 128],
                                                   acc[:, s, t, c * 128:c * 128 + 128], ident[:, :])
                    last.then_inc(tr_done, 1)

                def gram_mm(j, s, c):
                    base = b * 128 + j * 16 + 8 * s
                    pe.wait_ge(tr_evac, base + c + 1)
                    for h in range(HEADS):
                        qk = qkt[:, c % 2, h * 96:h * 96 + 96]
                        last = mm(ps[0:96, GR, h * 96:h * 96 + 96], qk, qk, start=False, stop=False, skip_group_check=True)
                    last.then_inc(gr_done, 1)

                def tg(j, s, first, last=False):
                    transposes(j, s, 0, first, last)
                    for c in range(1, 8):
                        transposes(j, s, c, first, last)
                        gram_mm(j, s, c - 1)
                    gram_mm(j, s, 7)

                def step(j, s):
                    conv1x1(j, s)
                    if has_y and isinstance(j, int) and j == 0 and s == 0:
                        attn_proj(b - 1)
                    conv_tile4(j, s)

                step(0, 0)
                def proj_of_last(j, s):
                    if has_y:
                        proj(b - 1, j, s, b * 81 + j * 10 + (5 * s + 1))

                proj_of_last(0, 0)
                step(0, 1)
                tg(0, 0, True)
                proj_of_last(0, 1)
                with pe.Fori(1, HB) as j:
                    step(j, 0)
                    tg(j - 1, 1, False)
                    proj_of_last(j, 0)
                    step(j, 1)
                    tg(j, 0, False)
                    proj_of_last(j, 1)
                pe.wait_ge(t4_evac, b1 * NBLK)
                if has_y:
                    group_norm(gy, b - 1)
                if has_next:
                    group_norm(gx, b + 1)
                tg(HB - 1, 1, False, True)

            images(pe, image)
            attn_transpose(NB - 1)
            attn_proj(NB - 1)
            proj(NB - 1, 0, 0)
            proj(NB - 1, 0, 1)
            with pe.Fori(1, HB) as j:
                for s in range(2):
                    proj(NB - 1, j, s)
            group_norm(gy, NB - 1)

            def stage_a(n, side, w):
                gp, ch = w
                pe.wait_ge(t0_done, n * 2 + side + 1)
                ge(pe, z1_done, n * 2 + side)
                for c in range(ch):
                    last = mm(ps[0:GP, PA + c, :], w1[:, gp, :], t0b[:, side, c * HALF:c * HALF + HALF])
                last.then_inc(a_done, 1)

            def stage_b(n, side, w):
                gp, ch = w
                pe.wait_ge(h1_done, n * 2 + side + 1)
                ge(pe, h2_done, n * 2 + side)
                for c in range(ch):
                    last = mm(ps[0:GP, PB + c, :], w2[:, gp, :], zb[:, side, c * HALF:c * HALF + HALF])
                last.then_inc(b_done, 1)

            def stage_c(n, side, w):
                gp, ch = w
                pe.wait_ge(h2_done, n * 2 + side + 1)
                ge(pe, up_done if side else lo_done, n)
                for c in range(ch):
                    last = mm(ps[0:GP, PC + side, :], w3[:, gp, c, :], hb[:, side, c * HALF:c * HALF + HALF], start=c == 0, stop=c == ch - 1)
                last.then_inc(c_done, 1)

            def body(gi, gp, it):
                n = gi * NIT + it
                w, w1_ = place(gi, gp, it), place(gi, gp, it - 1)
                stage_a(n, 0, w)
                if w1_:
                    stage_b(n - 1, 1, w1_)
                    stage_c(n - 1, 0, w1_)
                stage_a(n, 1, w)
                stage_b(n, 0, w)
                if w1_:
                    stage_c(n - 1, 1, w1_)

            def group(gi, gp):
                pe.wait_ge(mats_ready, gi + 1)
                body(gi, gp, 0)
                first = 1
                if isinstance(gi, int) and gi == 0:
                    body(0, 0, 1)
                    first = 2
                with pe.Fori(first, 10) as it:
                    body(gi, gp, it)
                body(gi, gp, 10)
                if isinstance(gi, int) and gi == NG - 1:
                    n = gi * NIT + NIT
                    stage_b(n - 1, 1, (gp, LASTC))
                    stage_c(n - 1, 0, (gp, LASTC))
                    stage_c(n - 1, 1, (gp, LASTC))

            groups(pe, group)

        @block.vector
        def _(dve):
            dve.wait_ge(w_loaded, 16 * 9)
            dve.wait_ge(zeroed, 2)
            for k in range(6):
                dx, blk = k % 3, k // 3
                for h in range(2):
                    for ho in range(2):
                        dy = 2 * blk + h - ho
                        if 0 <= dy < 3:
                            last = nc.vector.tensor_scalar(band[64 * h:64 * h + 64, k, 64 * ho:64 * ho + 64],
                                                           ident[64 * h:64 * h + 64, 64 * h:64 * h + 64],
                                                           dwc[64 * h:64 * h + 64, 4, 3 * dy + dx:3 * dy + dx + 1], None, ALU.mult)
            last.then_inc(band_ready, 1)

            def flat(ap):
                return ap.rearrange("p a s -> p (a s)")

            def group_stats(g, bs, b):
                nc.vector.memset(gs[:, 0, 0:1], 0.0).then_inc(g["mv_marked"], 1)
                nc.vector.bn_aggr(mv[:, 0, :], flat(bs[0][:, :, :]))
                nc.vector.bn_aggr(mv[:, 1, :], flat(bs[1][:, :, :])).then_inc(g["mv_ready"], 1)
                dve.wait_ge(g["mg_ready"], b + 1)
                nc.vector.tensor_tensor(gs[:, 0, :], mv[:, :, 0], ps[:, T4O, 0:2], ALU.subtract)
                nc.vector.tensor_scalar(gs[:, 5, :], ps[:, T4O, 0:2], -1.0, None, ALU.mult).then_inc(g["dev_ready"], 1)
                dve.wait_ge(g["dev_ready"], b + 1)
                nc.vector.tensor_tensor(gs[:, 1, :], gs[:, 0, :], gs[:, 0, :], ALU.mult).then_inc(g["dsq_ready"], 1)
                dve.wait_ge(g["dsq_ready"], b + 1)
                nc.vector.tensor_tensor(gs[:, 2, :], gs[:, 1, :], mv[:, :, 1], ALU.add).then_inc(g["q_ready"], 1)
                dve.wait_ge(g["vg_ready"], b + 1)
                nc.vector.tensor_scalar(gs[:, 3, :], ps[:, T4O, 2:4], GN_EPS, None, ALU.add).then_inc(g["ve_ready"], 1)
                dve.wait_ge(g["sd_ready"], b + 1)

            def x_norm(b):
                dve.wait_ge(st_done, b * NBLK + NBLK)
                group_stats(gx, sx_bs, b)
                nc.vector.reciprocal(gs[:, 1, :], gs[:, 4, :]).then_inc(gx["rstd_ready"], 1)
                dve.wait_ge(gx["rstd_ready"], b + 1)
                nc.vector.tensor_scalar(ws_a[:, :], wq_a[:, :], gs[:, 1, 0:1], None, ALU.mult)
                nc.vector.tensor_scalar(ws_b[:, :], wq_b[:, :], gs[0:CB, 1, 1:2], None, ALU.mult).then_inc(ws_ready, 1)

            def y_norm(b):
                dve.wait_ge(y_stats, b * NBLK + NBLK)
                group_stats(gy, sy_bs, b)
                for t in range(2):
                    nc.vector.tensor_scalar(rout[:, t, 0:1], gs[:, 5, t:t + 1], -1.0, None, ALU.mult)
                    last = nc.vector.reciprocal(rout[:, t, 1:2], gs[:, 4, t:t + 1])
                last.then_inc(gy["rstd_ready"], 1)

            def block_stats(bs, j, s, a, b_):
                for h in range(2):
                    i = j * 4 + (2 * s + h)
                    i = i if isinstance(i, int) else dve.snap(i)
                    nc.vector.bn_stats(flat(bs[0][:, at(i, 1), :]), a[:, s, h * HALF:h * HALF + HALF])
                i = j * 2 + s
                i = i if isinstance(i, int) else dve.snap(i)
                return nc.vector.bn_stats(flat(bs[1][:, at(i, 1), :]), b_[:, s, :])

            def x_stats(b, j, s):
                dve.wait_ge(sx_loaded[s], (b * HB + j) * 48 + 48)
                dve.wait_ge(zeroed, 2)
                block_stats(sx_bs, j, s, sxa, sxb).then_inc(st_done, 1)

            def proj(b, j, s, alone):
                n16 = b * NBLK + j * 2 + s
                ya, yb = y_banks(s, alone)
                dve.wait_ge(yx_loaded[s], (b * HB + j) * 48 + 48)
                oa, ob = (sxa, sxb) if alone else (yxa, yxb)
                if alone:
                    if not isinstance(j, int):
                        dve.wait_ge(x1_stored[s], (b * HB + j) * 48)
                    dve.wait_ge(ya_ready, n16 + 1)
                if alone:
                    nc.vector.tensor_tensor(oa[:, s, :].rearrange("p (a n) -> p a n", a=2), yxa[:, s, :].rearrange("p (a n) -> p a n", a=2),
                                            ps[:, ya:ya + 2, :], ALU.add).then_inc(ya_done, 1)
                dve.wait_ge(yb_ready, n16 + 1)
                nc.vector.tensor_tensor(ob[:, s, :], yxb[:, s, :], ps[:, yb, :], ALU.add).then_inc(yb_done, 1)
                dve.wait_ge(ya_done, n16 + 1)
                dve.wait_ge(yb_done, n16 + 1)
                dve.wait_ge(zeroed, 2)
                block_stats(sy_bs, j, s, oa, ob).then_inc(y_stats, 1)

            with dve.Fori(0, HB) as j:
                x_stats(0, j, 0)
                x_stats(0, j, 1)
            x_norm(0)

            def conv_tiles(b, j, s, tiles):
                tb = b * (NBLK * NT) + j * (2 * NT) + NT * s
                chain = (b * NBLK + j * 2 + s) * (NT * 8)
                k = 8 * tiles[0]
                for n, tap in enumerate(TAPS):
                    dy, dx = tap // 3, tap % 3
                    for t in tiles:
                        if n == 0:
                            dve.wait_ge(tap_done, tb + t + 1)
                        else:
                            dve.wait_ge(dw_chain, chain + (k + 1 - len(tiles)))
                        a = acc[:, s, t, :].rearrange("p (r w) -> p r w", w=W)
                        nc.vector.scalar_tensor_tensor(out=a, in0=pbuf[:, s, t, dy:dy + RB, dx:dx + W],
                                                       scalar=dwc[:, t, tap:tap + 1], in1=a,
                                                       op0=ALU.mult, op1=ALU.add).then_inc(dw_chain, 1)
                        k += 1

            def then(i, name, b):
                i.then_inc(A[name], 1)
                dve.wait_ge(A[name], b + 1)

            def attention(b, has_y):
                dve.wait_ge(gr_done, b * 128 + 128)
                then(nc.vector.tensor_copy(gram[:, :, :].rearrange("p h d -> p (h d)"), ps[0:96, GR, 0:384]), "gram", b)
                for h in range(HEADS):
                    last = nc.vector.tensor_tensor(gtmp[:, h, :], gram[:, h, :], ident[0:96, 0:96], ALU.mult)
                then(last, "diag", b)
                nc.vector.tensor_reduce(nrm[:, 0, :], gtmp[:, :, :], AX.X, ALU.add).then_inc(A["n2"], 1)
                dve.wait_ge(A["n"], b + 1)
                then(nc.vector.tensor_scalar(nrm[:, 2, :], nrm[:, 1, :], EPS, None, ALU.add), "ne", b)
                then(nc.vector.reciprocal(nrm[:, 3, :], nrm[:, 2, :]), "r1", b)
                then(nc.vector.tensor_tensor(nrm[:, 4, :], nrm[:, 1, :], nrm[:, 3, :], ALU.mult), "m", b)
                then(nc.vector.tensor_scalar(nrm[:, 5, :], nrm[:, 4, :], EPS, None, ALU.max), "m2", b)
                then(nc.vector.reciprocal(nrm[:, 6, :], nrm[:, 5, :]), "r2", b)
                then(nc.vector.tensor_tensor(nrm[:, 7, :], nrm[:, 3, :], nrm[:, 6, :], ALU.mult), "s", b)
                for h in range(HEADS):
                    last = nc.vector.tensor_scalar(gtmp[:, h, :], gram[:, h, :], nrm[:, 7, h:h + 1], None, ALU.mult)
                last.then_inc(A["rows"], 1)
                dve.wait_ge(A["tps"], b + 1)
                for h in range(HEADS):
                    last = nc.vector.tensor_scalar(att[:, 0, h, :], ps[0:CH, TR, h * 96 + CH:h * 96 + 96],
                                                   nrm[0:CH, 7, h:h + 1], tmp_bc[:, h:h + 1], ALU.mult, ALU.mult)
                then(last, "nq", b)
                then(nc.vector.tensor_reduce(nrm[0:CH, 0, :], att[:, 0, :, :], AX.X, ALU.max), "mx", b)
                for h in range(HEADS):
                    last = nc.vector.tensor_scalar(att[:, 1, h, :], att[:, 0, h, :], nrm[0:CH, 0, h:h + 1], None, ALU.subtract)
                last.then_inc(A["sub"], 1)
                if has_y:
                    dve.wait_ge(stat_stored, b * 32)
                dve.wait_ge(A["exp"], b + 1)
                then(nc.vector.tensor_reduce(nrm[0:CH, 1, :], att[:, 2, :, :], AX.X, ALU.add), "sum", b)
                then(nc.vector.reciprocal(nrm[0:CH, 2, :], nrm[0:CH, 1, :]), "rs", b)
                for h in range(HEADS):
                    last = nc.vector.tensor_scalar(apad[:, h, h * CH:h * CH + CH], att[:, 2, h, :], nrm[0:CH, 2, h:h + 1], None, ALU.mult)
                last.then_inc(A["pad"], 1)

            def attn_copy(b):
                dve.wait_ge(A["ptps"], b + 1)
                nc.vector.tensor_copy(pt_a[:, :], ps[:, TR + 1, 0:C])
                nc.vector.tensor_copy(pt_b[:, :], ps[0:CB, TR, 0:C]).then_inc(A["pt"], 1)

            def image(b, has_y, has_next):
                def turn(j, s, last=False):
                    conv_tiles(b, j, s, (0, 1))
                    first = has_y and isinstance(j, int) and j == 0 and s == 0
                    if first:
                        attn_copy(b - 1)
                        conv_tiles(b, j, s, (2,))
                    if has_y:
                        proj(b - 1, j, s, False)
                    if first:
                        conv_tiles(b, j, s, (3,))
                    elif last:
                        if has_next:
                            x_stats(b + 1, j, s)
                        if has_y:
                            y_norm(b - 1)
                        if has_next:
                            x_norm(b + 1)
                        conv_tiles(b, j, s, (2,))
                        conv_tiles(b, j, s, (3,))
                    else:
                        conv_tiles(b, j, s, (2, 3))
                    if has_next and not last:
                        x_stats(b + 1, j, s)

                turn(0, 0)
                turn(0, 1)
                with dve.Fori(1, HB - 1) as j:
                    turn(j, 0)
                    turn(j, 1)
                turn(HB - 1, 0)
                turn(HB - 1, 1, True)
                attention(b, has_y)

            images(dve, image)
            attn_copy(NB - 1)
            proj(NB - 1, 0, 0, True)
            proj(NB - 1, 0, 1, True)
            with dve.Fori(1, HB) as j:
                proj(NB - 1, j, 0, True)
                proj(NB - 1, j, 1, True)
            y_norm(NB - 1)

            dve.wait_ge(tab_loaded, 16)
            nc.vector.memset(w3[:, :, :, :], 0.0).then_inc(w3_zeroed, 1)
            dve.wait_ge(stats_loaded, 48)
            dve.wait_ge(tab_act, 2)
            n = [0]

            def link(i):
                n[0] += 1
                i.then_inc(lin_chain, 1)
                dve.wait_ge(lin_chain, n[0])

            def tt(o, a, b_, op):
                link(nc.vector.tensor_tensor(o, a, b_, op))

            link(nc.vector.tensor_scalar(sp_u[:, :, :], sp_e[:, :, :], 1.0, None, ALU.add))
            dve.wait_ge(tab_act, 3)
            link(nc.vector.tensor_scalar(sp_u[:, :, :], sp_u[:, :, :], 1.0, None, ALU.subtract))
            link(nc.vector.tensor_scalar(sp_m[:, :, :], sp_u[:, :, :], 0.0, None, ALU.is_equal))
            tt(sp_l[:, :, :], sp_l[:, :, :], sp_m[:, :, :], ALU.add)
            tt(sp_u[:, :, :], sp_u[:, :, :], sp_m[:, :, :], ALU.add)
            link(nc.vector.reciprocal(sp_m[:, :, :], sp_u[:, :, :]))
            tt(sp_l[:, :, :], sp_l[:, :, :], sp_m[:, :, :], ALU.mult)
            tt(sp_l[:, :, :], sp_l[:, :, :], sp_e[:, :, :], ALU.mult)
            link(nc.vector.scalar_tensor_tensor(out=tab[:, :, 0:24], in0=tab[:, :, 0:24], scalar=0.0, in1=sp_l[:, :, :], op0=ALU.max, op1=ALU.add))
            M0, M1, M2, M3, TF, B0, B1, B2, B3, ISF = 0, 3, 12, 21, 24, 27, 30, 33, 36, 37

            for f in range(3):
                tt(a0[:, :, f], tab[:, :, M0 + f], sta[:, :, 1], ALU.mult)
                tt(t3[:, :, f], a0[:, :, f], sta[:, :, 0], ALU.mult)
            tt(k0[:, :, :], tab[:, :, B0:B0 + 3], t3[:, :, :], ALU.subtract)
            for side, half in ((0, -0.5), (1, 0.5)):
                link(nc.vector.scalar_tensor_tensor(out=c0[:, :, side, :], in0=tab[:, :, M0:M0 + 3], scalar=half, in1=k0[:, :, :],
                                                    op0=ALU.mult, op1=ALU.add))

            def mix(o, m, v, off):
                for f in range(3):
                    tt(t3[:, :, f], m[:, :, f], v[:, :, f], ALU.mult)
                tt(t3[:, :, 0], t3[:, :, 0], t3[:, :, 1], ALU.add)
                if off is not None:
                    tt(t3[:, :, 0], t3[:, :, 0], off, ALU.add)
                tt(o, t3[:, :, 0], t3[:, :, 2], ALU.add)

            for o in range(3):
                mix(k0[:, :, o], tab[:, :, M1 + 3 * o:M1 + 3 * o + 3], a0[:, :, :], None)
            for side in range(2):
                for o in range(3):
                    mix(k1[:, :, side, o], tab[:, :, M1 + 3 * o:M1 + 3 * o + 3], c0[:, :, side, :], tab[:, :, B1 + o])
                for o in range(3):
                    mix(k2[:, :, side, o], tab[:, :, M2 + 3 * o:M2 + 3 * o + 3], k1[:, :, side, :], tab[:, :, B2 + o])
                mix(cc[:, :, K_C3 + side], tab[:, :, M3:M3 + 3], k2[:, :, side, :], tab[:, :, B3])

            def own(o, v):
                link(nc.vector.tensor_scalar(o, v[0], tab[:, 0, ISF:ISF + 1], None, ALU.mult))
                for f in (1, 2):
                    link(nc.vector.scalar_tensor_tensor(out=o, in0=v[f], scalar=tab[:, 0, ISF + f:ISF + f + 1], in1=o,
                                                        op0=ALU.mult, op1=ALU.add))

            own(cc[:, :, K_S0], [a0[:, :, f] for f in range(3)])
            own(cc[:, :, K_O0:K_O0 + 2], [c0[:, :, :, f] for f in range(3)])
            own(cc[:, :, K_A1], [k0[:, :, f] for f in range(3)])
            own(cc[:, :, K_C1:K_C1 + 2], [k1[:, :, :, f] for f in range(3)])
            own(cc[:, :, K_C2:K_C2 + 2], [k2[:, :, :, f] for f in range(3)])
            own(cc[:, :, K_W1:K_W1 + 3], [tab[:, :, M1 + f:M1 + 9:3] for f in range(3)])
            own(cc[:, :, K_M2:K_M2 + 3], [tab[:, :, M2 + f:M2 + 9:3] for f in range(3)])
            own(cc[:, :, K_M3], [tab[:, :, M3 + f] for f in range(3)])
            for o in range(3):
                tt(cc[:, :, K_W1 + o], cc[:, :, K_W1 + o], tab[:, :, TF], ALU.mult)
            link(nc.vector.tensor_copy(cc[:, :, K_F1:K_F1 + 2], tab[:, :, TF + 1:TF + 3]))

            def prepare(gi, gp):
                g0 = gi if isinstance(gi, int) else dve.snap(gi)
                if not (isinstance(gi, int) and gi < 2):
                    dve.wait_ge(res_all, gi * NIT - NIT)
                dve.wait_ge(w3_zeroed, 1)
                nc.vector.tensor_copy(cur[:, gp, :], flat(cc[:, at(g0, 1), :])).then_inc(cur_ready, 1)
                dve.wait_ge(cur_ready, gi + 1)
                for o in range(3):
                    c = slice(o * G, o * G + G)
                    nc.vector.tensor_scalar(w1[:, gp, c], diag[:, :], cur[:, gp, K_W1 + o:K_W1 + o + 1], None, ALU.mult)
                    nc.vector.tensor_scalar(w2[:, gp, c], diag[:, :], cur[:, gp, K_M2 + o:K_M2 + o + 1], None, ALU.mult)
                    last = nc.vector.tensor_scalar(w3[:, gp, o, c], diag[:, :], cur[:, gp, K_M3:K_M3 + 1], None, ALU.mult)
                last.then_inc(mats_ready, 1)

            def cols(ap, ch):
                return ap[:, 0:ch * HALF].rearrange("p (a n) -> p a n", n=HALF)

            def z1(n, side, par, w):
                gp, ch = w
                u = n * 2 + side
                dve.wait_ge(a_done, u + 1)
                ge(dve, b_done, u - 1)
                nc.vector.scalar_tensor_tensor(out=cols(zb[:, side, :], ch), in0=cols(xr[:, par, :], ch), scalar=cur[:, gp, K_A1:K_A1 + 1],
                                               in1=ps[0:GP, PA:PA + ch, :], op0=ALU.mult, op1=ALU.add).then_inc(z1_done, 1)

            def h1(n, side, w):
                gp, ch = w
                dve.wait_ge(t1_done, n * 2 + side + 1)
                m = ch * HALF
                nc.vector.scalar_tensor_tensor(out=zb[:, side, 0:m], in0=t12[:, side, 0:m], scalar=cur[:, gp, K_F1:K_F1 + 1],
                                               in1=zb[:, side, 0:m], op0=ALU.mult, op1=ALU.add).then_inc(h1_done, 1)

            def h2(n, side, w):
                gp, ch = w
                u = n * 2 + side
                dve.wait_ge(t2_done, u + 1)
                ge(dve, c_done, u - 1)
                nc.vector.scalar_tensor_tensor(out=cols(hb[:, side, :], ch), in0=cols(t12[:, side, :], ch),
                                               scalar=cur[:, gp, K_F2:K_F2 + 1], in1=ps[0:GP, PB:PB + ch, :],
                                               op0=ALU.mult, op1=ALU.add).then_inc(h2_done, 1)

            def fin_lo(n, w):
                dve.wait_ge(c_done, n * 2 + 1)
                ge(dve, sl_done, n)
                ge(dve, sum_done, n)
                nc.vector.tensor_scalar(lo_c[:, :], ps[0:GP, PC, :], cur[:, w[0], K_C3:K_C3 + 1], None, ALU.add).then_inc(lo_done, 1)

            def fin_sl(n):
                dve.wait_ge(sgn_done, n + 1)
                ge(dve, sig_done, n)
                nc.vector.tensor_tensor(sul[:, 0, :], lo_c[:, :], sgn[:, :], ALU.mult).then_inc(sl_done, 1)

            def fin_res(n, par):
                dve.wait_ge(xd_loaded[par], (n - par) * 24 + 48)
                ge(dve, res_stored[par], (n - par) * 24)
                dve.wait_ge(lik_done, n + 1)
                nc.vector.scalar_tensor_tensor(out=res[:, par, :], in0=lik[:, :], scalar=BOUND, in1=xd[:, par, :],
                                               op0=ALU.max, op1=ALU.add).then_inc(res_all, 1)

            def body(gi, gp, it, par):
                n = gi * NIT + it
                w, w1_, w2_, w3_ = (place(gi, gp, i) for i in (it, it - 1, it - 2, it - 3))
                if w2_:
                    fin_lo(n - 2, w2_)
                z1(n, 0, par, w)
                if w3_:
                    fin_res(n - 3, 1 - par)
                h1(n, 0, w)
                if w1_:
                    h2(n - 1, 1, w1_)
                if w2_:
                    fin_sl(n - 2)
                z1(n, 1, par, w)
                h1(n, 1, w)
                h2(n, 0, w)

            def group(gi, gp):
                if isinstance(gi, int) and gi == 0:
                    prepare(0, 0)
                    dve.wait_ge(mats_ready, 1)
                body(gi, gp, 0, gp)
                body(gi, gp, 1, 1 - gp)
                first = 1
                if isinstance(gi, int) and gi == 0:
                    body(0, 0, 2, 0)
                    body(0, 0, 3, 1)
                    body(0, 0, 4, 0)
                    body(0, 0, 5, 1)
                    first = 3
                with dve.Fori(first, 5) as p:
                    body(gi, gp, 2 * p, gp)
                    body(gi, gp, 2 * p + 1, 1 - gp)
                if not (isinstance(gi, int) and gi == NG - 1):
                    prepare(gi + 1, 1 - gp)
                body(gi, gp, 10, gp)
                if isinstance(gi, int) and gi == NG - 1:
                    n = gi * NIT + NIT
                    fin_lo(n - 2, (gp, 3))
                    fin_res(n - 3, gp)
                    h2(n - 1, 1, (gp, LASTC))
                    fin_sl(n - 2)
                    fin_res(n - 2, 1 - gp)
                    fin_lo(n - 1, (gp, LASTC))
                    fin_sl(n - 1)
                    fin_res(n - 1, gp)

            groups(dve, group)


_W = "L0_conv_"
_E = "L1_conv_"


def lay_out(inputs):
    import numpy as np
    f = {k: np.asarray(v) for k, v in inputs.items()}
    a = {"x": np.ascontiguousarray(f["x"]).reshape(ROWS, NPX)}
    order = np.concatenate([np.arange(CH) + h * CH + part * C for h in range(HEADS) for part in range(2)] + [np.arange(2 * C, 3 * C)])
    wt = f[_W + "w_qkv"][order].T
    a["wqkv"] = np.concatenate([wt, wt[:, 512:576]], axis=1)
    wd = f[_W + "w_dw"].reshape(3 * C, 9)[order]
    a["wdw"] = np.stack([wd[0:128], wd[128:256], wd[256:384], wd[384:512], np.concatenate([wd[512:576], wd[512:576]])], axis=1)
    a["wproj"] = f[_W + "w_proj"].T.reshape(HEADS, CH, C).transpose(1, 0, 2)
    a["temp"] = np.tile(f[_W + "temperature"].reshape(1, HEADS), (CH, 1))
    lies = np.concatenate([np.arange(C), np.arange(CA, C)])
    part = np.where(lies < CA, 1.0, 0.5) / 6.0
    a["grp"] = (lies[:, None] // 6 == lies[None, :] // 6) * part[:, None].astype(np.float32)
    a["ident"] = np.eye(128, dtype=np.float32)
    a["diag"] = np.tile(np.eye(G, dtype=np.float32), (3, 1))
    cols = []
    for own in range(3):
        m = [f[_E + "m0"][:, fl, 0] for fl in range(3)]
        m += [f[_E + "m1"][:, o, fl] for o in range(3) for fl in range(3)]
        m += [f[_E + "m2"][:, o, fl] for o in range(3) for fl in range(3)]
        m += [f[_E + "m3"][:, 0, fl] for fl in range(3)]
        m += [f[_E + f"f{i}"][:, own, 0] for i in range(3)]
        m += [f[_E + f"b{i}"][:, fl, 0] for i in range(3) for fl in range(3)] + [f[_E + "b3"][:, 0, 0]]
        rows = np.tile(np.stack(m, axis=1), (NB, 1))
        rows = np.concatenate([rows, np.zeros((NG * G - ROWS, rows.shape[1]), np.float32)])
        is_f = np.zeros((NG * G, 4), np.float32)
        is_f[:, own] = 1.0
        rows = np.concatenate([rows, is_f], axis=1)
        cols.append(rows.reshape(NG, G, NIN).transpose(1, 0, 2))
    a["par"] = np.concatenate(cols)
    return {k: np.ascontiguousarray(v) for k, v in a.items()}


_INS = ["x", "wqkv", "wdw", "wproj", "temp", "grp", "ident", "diag", "par"]


def kernel(**inputs):
    import concourse.bacc as _bacc
    from concourse import mybir as _mybir
    from concourse.bass_utils import run_bass_kernel_spmd as _run

    nc = _bacc.Bacc("TRN2", target_bir_lowering=False, num_devices=1)
    laid = lay_out(inputs)
    arrays, args = {}, []
    for name in _INS:
        a = laid[name]
        arrays[f"in_{name}_dram"] = a
        args.append(nc.dram_tensor(f"in_{name}_dram", a.shape, _mybir.dt.from_np(a.dtype), kind="ExternalInput").ap())
    args.append(nc.dram_tensor("out_0_dram", (ROWS, NPX), _mybir.dt.float32, kind="ExternalOutput").ap())
    build(nc, *args)
    r = _run(nc, [arrays], core_ids=[0])
    return r.results[0]["out_0_dram"].reshape(NB, C, H, W)
```
